# Optimizing a Trainium2 kernel written in Bass

```python
import numpy as np
import jax
import jax.numpy as jnp

def _softmax(x, axis=-1):
    return jax.nn.softmax(x, axis=axis)

def _gelu(x):
    return jax.nn.gelu(x, approximate=True)

def _silu(x):
    return jax.nn.silu(x)

def _sigmoid(x):
    return jax.nn.sigmoid(x)

def _layernorm(x, axis=-1, eps=1e-05):
    m = jnp.mean(x, axis=axis, keepdims=True)
    v = jnp.var(x, axis=axis, keepdims=True)
    return (x - m) / jnp.sqrt(v + eps)

def _scatter_add(tgt, idx, src, axis=0):
    return tgt.at[idx].add(src)

def _segment_sum(src, seg, n):
    return jax.ops.segment_sum(src, seg, n)
kernel_name = 'mk_cond_resid_d2_seqx_r8_f7ff6c'

def setup_inputs(seed: int=0):
    np.random.seed(seed)
    _w = jnp.asarray

    def _rec_inputs():
        import jax
        import jax.numpy as jnp
        _rk = jax.random.key(seed)
        x = -0.0003929 + 0.9999 * jax.random.normal(jax.random.fold_in(_rk, 1), (128, 32, 512), jnp.float32)
        _lenS = 32 - jax.random.randint(jax.random.fold_in(_rk, 7), (128,), 0, max(1, 32 // 4) + 1, jnp.int32)
        _lenS2 = 32 - jax.random.randint(jax.random.fold_in(_rk, 8), (128,), 0, max(1, 32 // 4) + 1, jnp.int32)
        itok_B_78_3631 = jax.random.randint(jax.random.fold_in(_rk, 11), (128,), 78, 454, jnp.int32)
        itok_B_2_6 = jax.random.randint(jax.random.fold_in(_rk, 12), (128,), 2, 7, jnp.int32)
        return (x, itok_B_78_3631, itok_B_2_6)
    x, itok_B_78_3631, itok_B_2_6 = _rec_inputs()

    def _L0_cond_setup():
        import math
        import jax, jax.numpy as jnp
        import numpy as np
        B, H, N, L = (16, 32, 64, 512)
        DT_MIN, DT_MAX = (0.001, 0.1)

        def _get_kernel(log_dt, C, log_A_real, A_imag, length):
            dt = jnp.exp(log_dt)
            Cc = C[..., 0] + 1j * C[..., 1]
            A = -jnp.exp(log_A_real) + 1j * A_imag
            dtA = A * dt[:, None]
            Ct = Cc * (jnp.exp(dtA) - 1.0) / A
            P = dtA[:, :, None] * jnp.arange(length, dtype=jnp.float32)
            K = 2.0 * jnp.einsum('hn,hnl->hl', Ct, jnp.exp(P)).real
            return K
        key = jax.random.key(seed)
        ks = jax.random.split(key, 5)
        u = jax.random.normal(ks[0], (B, H, L), dtype=jnp.float32)
        log_dt = jax.random.uniform(ks[1], (H,), dtype=jnp.float32) * (math.log(DT_MAX) - math.log(DT_MIN)) + math.log(DT_MIN)
        C = jax.random.normal(ks[2], (H, N, 2), dtype=jnp.float32)
        log_A_real = jnp.log(0.5 * jnp.ones((H, N), dtype=jnp.float32))
        A_imag = math.pi * jnp.broadcast_to(jnp.arange(N, dtype=jnp.float32), (H, N))
        D = jax.random.normal(ks[3], (H,), dtype=jnp.float32)
        length = jax.random.randint(ks[4], (B,), 1, L + 1, dtype=jnp.int32)
        return {'u': u, 'log_dt': log_dt, 'C': C, 'log_A_real': log_A_real, 'A_imag': A_imag, 'D': D, 'length': length}
    _L0_cond_all = _L0_cond_setup()
    _L0_cond_in = {k: v for k, v in _L0_cond_all.items() if k in ('log_dt', 'C', 'log_A_real', 'A_imag', 'D')}
    del _L0_cond_all

    def _L1_cond_setup():
        import jax, jax.numpy as jnp
        import numpy as np
        B, N, H, F = (4, 64, 512, 1376)
        L, R, RANK = (1, 16, 16)
        SCALE = 0.5
        key = jax.random.key(seed)
        ks = jax.random.split(key, 12)
        nrm = lambda k, shape, fan: jax.random.normal(k, shape, jnp.float32) * fan ** (-0.5)
        inp = {'x': jax.random.normal(ks[0], (B, N, H), jnp.float32), 'W_gate': nrm(ks[1], (F, H), H), 'W_up': nrm(ks[2], (F, H), H), 'W_down': nrm(ks[3], (H, F), F), 'A_gate': nrm(ks[4], (L, R, RANK, H), H), 'B_gate': nrm(ks[5], (L, R, F, RANK), RANK), 'A_up': nrm(ks[6], (L, R, RANK, H), H), 'B_up': nrm(ks[7], (L, R, F, RANK), RANK), 'A_down': nrm(ks[8], (L, R, RANK, F), F), 'B_down': nrm(ks[9], (L, R, H, RANK), RANK), 'lora_indices': jax.random.randint(ks[10], (B,), 0, R), 'layer_idx': 0}
        return inp
    _L1_cond_all = _L1_cond_setup()
    _L1_cond_in = {k: v for k, v in _L1_cond_all.items() if k in ('W_gate', 'W_up', 'W_down', 'A_gate', 'B_gate', 'A_up', 'B_up', 'A_down', 'B_down')}
    del _L1_cond_all
    return {'x': x, 'itok_B_78_3631': itok_B_78_3631, 'itok_B_2_6': itok_B_2_6, 'L0_cond_log_dt': _L0_cond_in['log_dt'], 'L0_cond_C': _L0_cond_in['C'], 'L0_cond_log_A_real': _L0_cond_in['log_A_real'], 'L0_cond_A_imag': _L0_cond_in['A_imag'], 'L0_cond_D': _L0_cond_in['D'], 'L1_cond_W_gate': _L1_cond_in['W_gate'], 'L1_cond_W_up': _L1_cond_in['W_up'], 'L1_cond_W_down': _L1_cond_in['W_down'], 'L1_cond_A_gate': _L1_cond_in['A_gate'], 'L1_cond_B_gate': _L1_cond_in['B_gate'], 'L1_cond_A_up': _L1_cond_in['A_up'], 'L1_cond_B_up': _L1_cond_in['B_up'], 'L1_cond_A_down': _L1_cond_in['A_down'], 'L1_cond_B_down': _L1_cond_in['B_down']}

def reference(x, itok_B_78_3631, itok_B_2_6, L0_cond_log_dt, L0_cond_C, L0_cond_log_A_real, L0_cond_A_imag, L0_cond_D, L1_cond_W_gate, L1_cond_W_up, L1_cond_W_down, L1_cond_A_gate, L1_cond_B_gate, L1_cond_A_up, L1_cond_B_up, L1_cond_A_down, L1_cond_B_down):
    import jax
    import jax.numpy as jnp

    def _L0_cond_ref(u, log_dt, C, log_A_real, A_imag, D, length):
        import math
        import jax, jax.numpy as jnp
        import numpy as np
        B, H, N, L = (16, 32, 64, 512)
        DT_MIN, DT_MAX = (0.001, 0.1)

        def _get_kernel(log_dt, C, log_A_real, A_imag, length):
            dt = jnp.exp(log_dt)
            Cc = C[..., 0] + 1j * C[..., 1]
            A = -jnp.exp(log_A_real) + 1j * A_imag
            dtA = A * dt[:, None]
            Ct = Cc * (jnp.exp(dtA) - 1.0) / A
            P = dtA[:, :, None] * jnp.arange(length, dtype=jnp.float32)
            K = 2.0 * jnp.einsum('hn,hnl->hl', Ct, jnp.exp(P)).real
            return K
        Bq, Hq, Lq = u.shape
        K = _get_kernel(log_dt, C, log_A_real, A_imag, Lq)
        n = 2 * Lq
        kf = jnp.fft.rfft(K, n=n)
        uf = jnp.fft.rfft(u, n=n)
        y = jnp.fft.irfft(uf * kf[None], n=n)[..., :Lq]
        y = y + u * D[:, None]
        mask = (jnp.arange(Lq)[None, :] < length[:, None]).astype(u.dtype)
        return y * mask[:, None, :]

    def _L1_cond_ref(x, W_gate, W_up, W_down, A_gate, B_gate, A_up, B_up, A_down, B_down, lora_indices, layer_idx):
        import jax, jax.numpy as jnp
        import numpy as np
        B, N, H, F = (4, 64, 512, 1376)
        L, R, RANK = (1, 16, 16)
        SCALE = 0.5

        def lora_add(base, inp, A, B):
            Ab = A[layer_idx][lora_indices]
            Bb = B[layer_idx][lora_indices]
            t = jnp.einsum('bri,bni->bnr', Ab, inp)
            return base + jnp.einsum('bor,bnr->bno', Bb, t) * SCALE
        gate = lora_add(jnp.einsum('bnh,fh->bnf', x, W_gate), x, A_gate, B_gate)
        up = lora_add(jnp.einsum('bnh,fh->bnf', x, W_up), x, A_up, B_up)
        act = jax.nn.silu(gate) * up
        down = lora_add(jnp.einsum('bnf,hf->bnh', act, W_down), act, A_down, B_down)
        return down
    x = x + _L0_cond_ref(x, L0_cond_log_dt, L0_cond_C, L0_cond_log_A_real, L0_cond_A_imag, L0_cond_D, itok_B_78_3631)
    x = x + _L1_cond_ref(x, L1_cond_W_gate, L1_cond_W_up, L1_cond_W_down, L1_cond_A_gate, L1_cond_B_gate, L1_cond_A_up, L1_cond_B_up, L1_cond_A_down, L1_cond_B_down, itok_B_2_6, 0)
    return x

_drawn_inputs = setup_inputs


def setup_inputs(seed=0):
    import zlib

    import numpy as np

    out = dict(_drawn_inputs(seed))
    spreads = {'L0_cond_log_A_real': (-0.6931471824645996, 0.2)}
    factors = {}
    for name, (base, spread) in spreads.items():
        noise = np.random.default_rng([zlib.crc32(name.encode()), seed]).standard_normal(out[name].shape)
        drawn = base * np.exp(spread * noise) if base else spread * noise
        out[name] = jnp.asarray(drawn.astype(out[name].dtype))
    for name, factor in factors.items():
        out[name] = (out[name] * factor).astype(out[name].dtype)
    return out
```

```python
from contextlib import ExitStack

import concourse.bass as bass
from concourse import mybir

F32 = mybir.dt.float32
F16 = mybir.dt.float16
I32 = mybir.dt.int32
ALU = mybir.AluOpType
ACT = mybir.ActivationFunctionType

P = 128
NB, NH, NL = 128, 32, 512
NST = 64
FF = 1376
R = 16
NAD = 16
KL = NL // P
FT = (FF + P - 1) // P
FLAST = FF - (FT - 1) * P
FH0 = 6 * P
FH1 = FF - FH0
FHS = [FH0, FH1]
CA, CC = 16, 32
KROW = NL + P
NW = 2 * KL * FF + FT * NL
WD0 = 2 * KL * FF
WCH = NW // NH
TB = 8
NT = NB // TB
TOK = TB * NH
Q = TOK // P
assert NW % NH == 0

S_X, S_W, S_T, S_ACT, S_T2 = 8.0, 256.0, 4.0, 4.0, 2.0
G_SCALE = S_X * S_W
O_SCALE = S_ACT * S_W
assert S_T * S_W == 0.5 * G_SCALE and S_T2 * S_W == 0.5 * O_SCALE

TWO_PI = 6.283185307179586
PI_HI, PI_MID = 6.28125, 0.0019350051879882812
PI_LO = TWO_PI - PI_HI - PI_MID
LN2 = 0.6931471805599453
LN2_HI = 0.693145751953125
LN2_LO = LN2 - LN2_HI
MAGIC = 12582912.0
EXP_C = [1 / 5040, 1 / 720, 1 / 120, 1 / 24, 1 / 6, 0.5, 1.0, 1.0]

NLA = 2 * KL * R * NAD // 2
LPARTS = [("A", h, NLA) for h in range(2)]
LPARTS += [("B", (blk, gu), FF) for blk in range(2) for gu in range(2)]
LPARTS += [("Ad", g, 4 * FT * R) for g in range(4)]
LPARTS += [("Bd", blk, NL) for blk in range(2)]
NLO = sum(n for _, _, n in LPARTS)


def build(nc, xt, wall, lora, ldt, lar, aim, cst, dvec, length, adapter, out):
    ctx = ExitStack()
    with ctx:
        def sb(name, shape, dt):
            return ctx.enter_context(nc.sbuf_tensor(name, shape, dt))

        def sem(name):
            return ctx.enter_context(nc.semaphore(name))

        krev = nc.dram_tensor("krev", [NH, KROW], F32, kind="Internal").ap()
        a_scr = nc.dram_tensor("a_scr", [NAD, P, 2, 2 * KL * R], F16, kind="Internal").ap()
        b_scr = nc.dram_tensor("b_scr", [NAD, 3, R, 2, FF], F16, kind="Internal").ap()
        ad_scr = nc.dram_tensor("ad_scr", [NAD, P, 2, FT * R], F16, kind="Internal").ap()
        bd_scr = nc.dram_tensor("bd_scr", [NAD, 2, R, 2, NL], F16, kind="Internal").ap()

        w_hi = sb("w_hi", [P, NW], F16)
        w_lo = sb("w_lo", [P, NW], F16)
        x1 = sb("x1", [P, KL, NH, NB], F32)
        up_lora = sb("up_lora", [P, 4 * 2 * FF], F16)
        lora_in = [up_lora[:, 4 * FF * i:4 * FF * i + 2 * FF].bitcast(F32) for i in range(2)]
        lora_hi = [up_lora[:, 4 * FF * i + 2 * FF:4 * FF * i + 3 * FF] for i in range(2)]
        lora_lo = [up_lora[:, 4 * FF * i + 3 * FF:4 * FF * i + 4 * FF] for i in range(2)]
        b_half = [up_lora[:, 0:8 * FH0].rearrange("p (j g f) -> p j g f", j=4, g=2),
                  up_lora[:, 8 * FH0:8 * FF].rearrange("p (j g f) -> p j g f", j=4, g=2)]
        a_buf = sb("a_buf", [P, TB, 2, KL, 2 * R], F16)
        ad_buf = sb("ad_buf", [P, TB, 2, FT, R], F16)
        bd_buf = sb("bd_buf", [P, Q, 2, NL], F16)
        xstage = sb("xstage", [P, 2, 2, KL, TB, NH], F16)
        wring = sb("wring", [P, 4, WCH], F32)
        act_hl = sb("act_hl", [P, FT, 2, TOK], F16)
        s_ring = act_hl[:, :, :, :].rearrange("p m e t -> p (m e t)")[:, 0:4 * 2 * NL].bitcast(F32)\
            .rearrange("p (s n) -> p s n", s=4)
        toep = xstage[:, 0].rearrange("p e k b h -> p (e k b h)").bitcast(F32).rearrange("p (s n) -> p s n", s=2)
        t_mov = sb("t_mov", [P, 2, 2, Q, P], F16)
        sg = sb("sg", [P, 2, TOK], F32)
        af = sb("af", [P, 2, TOK], F32)
        out_sb = sb("out_sb", [P, Q, NL], F32)
        mask = sg[:].rearrange("p a n -> p (a n)").rearrange("p (k b) -> p k b", k=KL)
        ym = out_sb
        sel = sb("sel", [P, Q * 2, R], F32)
        val = sb("val", [P, Q * 2, 3, R], F16)
        tt = sb("tt", [P, Q * 2, 2, 3 * R], F16)
        t2 = sb("t2", [P, Q, P], F16)
        t2a = sb("t2a", [P, Q, P], F16)
        ident = sb("ident", [P, P], F16)
        ident_x = sb("ident_x", [P, P], F16)
        pair_sel = sb("pair_sel", [P, 2], F32)
        half_pi = sb("half_pi", [P, 1], F32)

        wf = [w_hi[:, :].bitcast(F32), w_lo[:, :].bitcast(F32)]
        NE = CA + CC + 1
        NX = NH * NE

        def tmp(i, n0, shape):
            n = 1
            for s in shape:
                n *= s
            v = wf[i][:, n0:n0 + n]
            if len(shape) == 2:
                v = v.rearrange("p (a b) -> p a b", a=shape[0])
            return v

        theta = tmp(0, 0, [NH, NE])
        turns = tmp(0, NX, [NH, NE])
        sin_t = tmp(0, 2 * NX, [NH, NE])
        cos_t = tmp(0, 3 * NX, [NH, NE])
        mag_t = tmp(0, 4 * NX, [NH, NE])
        tab1 = tmp(1, 0, [NH, NE])
        tab2 = tmp(1, NX, [NH, NE])
        g1 = tmp(1, 2 * NX, [NH, CA])
        g2 = tmp(1, 2 * NX + NH * CA, [NH, CA])
        drow = tmp(1, 2 * NX + 2 * NH * CA, [NH, CC])
        ksb = tmp(1, 2 * NX + 2 * NH * CA + NH * CC, [NH, CC])
        at1 = 2 * NX + 2 * NH * CA + 2 * NH * CC
        lags = wf[1][:, at1:at1 + NE]
        ioti = wf[1][:, at1 + 64:at1 + 64 + KL * NB]
        leni = wf[1][:, at1 + 64 + KL * NB:at1 + 64 + KL * NB + NB].bitcast(I32)
        lenf = wf[1][:, at1 + 64 + KL * NB + NB:at1 + 64 + KL * NB + 2 * NB]
        at1 += 64 + KL * NB + 2 * NB
        zrow = wf[1][0:NH, at1:at1 + P]
        onehot = wf[1][0:1, at1 + P:at1 + P + CA]
        dval = wf[1][0:1, at1 + P + CA:at1 + P + CA + NH]
        small0 = at1 + P + CA + NH
        s0 = [0]

        def col(n=NH):
            s0[0] += n
            assert small0 + s0[0] <= NW // 2
            return wf[1][:, small0 + s0[0] - n:small0 + s0[0]]
        ex_in, ex_k, ex_r, ex_p, ex_o = [col(2 * NH) for _ in range(5)]
        a_im, c_re, c_im, a_re, d_re, d_im, e_re, e_im, w_re, w_im, den, ct_re, ct_im, u1, u2, coef_p, coef_q = \
            [col() for _ in range(17)]

        ps = ctx.enter_context(nc.psum_tensor("ps", [P, 8, 512], F32))

        s_par = sem("s_par")
        s_x = sem("s_x")
        s_pool = sem("s_pool")
        s_v = sem("s_v")
        s_a = sem("s_a")
        s_k = sem("s_k")
        s_kd = sem("s_kd")
        assert FT % 2 == 1
        HB = 4
        s_s = [sem(f"s_s{i}") for i in range(HB)]
        s_r = sem("s_r")
        s_w = [sem(f"s_w{i}") for i in range(HB)]
        s_y = sem("s_y")
        s_ym = sem("s_ym")
        s_x1 = sem("s_x1")
        s_wh = sem("s_wh")
        s_wl = sem("s_wl")
        s_li = [sem(f"s_li{i}") for i in range(2)]
        s_lc = sem("s_lc")
        s_lo = [sem(f"s_lo{i}") for i in range(2)]
        s_ga = sem("s_ga")
        s_gb = [sem(f"s_gb{i}") for i in range(2)]
        s_gad = sem("s_gad")
        s_gbd = sem("s_gbd")
        s_xh = sem("s_xh")
        s_xl = sem("s_xl")
        s_ta = sem("s_ta")
        s_tt = sem("s_tt")
        s_tp = sem("s_tp")
        s_tm = sem("s_tm")
        s_sel = sem("s_sel")
        s_val = sem("s_val")
        s_t2h = sem("s_t2h")
        s_gu = sem("s_gu")
        s_sg = sem("s_sg")
        s_af = sem("s_af")
        s_ah = sem("s_ah")
        s_al = sem("s_al")
        s_d = sem("s_d")
        s_t2 = sem("s_t2")
        s_t2p = sem("s_t2p")
        s_t2a = sem("s_t2a")
        s_acc = sem("s_acc")
        s_ev0 = sem("s_ev0")
        s_ev1 = sem("s_ev1")
        s_out = sem("s_out")

        def wait(eng, s, v):
            if not isinstance(v, int) or v > 0:
                eng.wait_ge(s, v)

        block = ctx.enter_context(nc.Block())
        NPAR = 11

        N_STORE = {"A": 2, "B": 3, "Ad": 2, "Bd": 4}
        STORES = []
        for i, (kind, _, _) in enumerate(LPARTS):
            STORES.append((STORES[i - 2] if i >= 2 else 0) + N_STORE[kind])

        V_STEP = {}
        V_KSB = [0]

        def vector_part_a(dve, v):
            n = [0]

            def step(ins, name=None):
                n[0] += 1
                ins.then_inc(s_v, 1)
                dve.wait_ge(s_v, n[0])
                if name:
                    V_STEP[name] = n[0]

            def exp_poly(x, k, r, p, o):
                step(v.tensor_scalar(k, x, 1 / LN2, -125.0, ALU.mult, ALU.max))
                step(v.tensor_scalar(k, k, 126.0, MAGIC, ALU.min, ALU.add))
                step(v.tensor_scalar(k, k, MAGIC, None, ALU.subtract))
                step(v.scalar_tensor_tensor(r, k, -LN2_HI, x, ALU.mult, ALU.add))
                step(v.scalar_tensor_tensor(r, k, -LN2_LO, r, ALU.mult, ALU.add))
                step(v.tensor_scalar(p, r, EXP_C[0], None, ALU.mult))
                for c in EXP_C[1:-1]:
                    step(v.scalar_tensor_tensor(p, p, c, r, ALU.add, ALU.mult))
                step(v.tensor_scalar(o.bitcast(I32), k, 127.0, 8388608.0, ALU.add, ALU.mult))
                step(v.scalar_tensor_tensor(o, p, 1.0, o, ALU.add, ALU.mult))

            def bc(x, m):
                return x.unsqueeze(2).to_broadcast([x.shape[0], NH, m])

            dve.wait_ge(s_par, 16 * NPAR)
            dve.wait_ge(s_pool, 12)
            step(v.tensor_copy(lenf, leni))
            step(v.tensor_tensor(mask, lenf.unsqueeze(1).to_broadcast([P, KL, NB]),
                                 ioti.rearrange("p (k b) -> p k b", k=KL), ALU.is_gt))
            step(v.memset(drow[0:1], 0.0))
            step(v.tensor_copy(drow[0:1, :, CC - 1], dval))
            step(v.memset(tt[:], 0.0))
            step(v.memset(pair_sel[:], 0.0))
            for b in range(4):
                step(v.memset(pair_sel[32 * b:32 * b + 32, b % 2:b % 2 + 1], 1.0))
            step(v.memset(t2[:], 0.0))
            exp_poly(ex_in, ex_k, ex_r, ex_p, ex_o)
            dt = ex_o[:, 0:NH]
            step(v.tensor_tensor(d_im, a_im, dt, ALU.mult))
            lagb = lags.unsqueeze(1).to_broadcast([P, NH, NE])
            step(v.tensor_tensor(theta, bc(d_im, NE), lagb, ALU.mult))
            step(v.tensor_scalar(turns, theta, 1 / TWO_PI, MAGIC, ALU.mult, ALU.add))
            step(v.tensor_scalar(turns, turns, MAGIC, None, ALU.subtract))
            for c in (PI_HI, PI_MID, PI_LO):
                step(v.scalar_tensor_tensor(theta, turns, -c, theta, ALU.mult, ALU.add))
            step(v.tensor_scalar(theta, theta, 3.1415925, -3.1415925, ALU.min, ALU.max), "theta")
            step(v.scalar_tensor_tensor(turns, theta, -1.0, theta, ALU.mult, ALU.max), "abs_theta")
            step(v.tensor_scalar(a_re, ex_o[:, NH:2 * NH], -1.0, None, ALU.mult))
            step(v.tensor_tensor(d_re, a_re, dt, ALU.mult))
            step(v.tensor_tensor(mag_t, bc(d_re, NE), lagb, ALU.mult), "mag")
            exp_poly(d_re, ex_k[:, 0:NH], ex_r[:, 0:NH], ex_p[:, 0:NH], ex_o[:, 0:NH])
            dve.wait_ge(s_a, 3)
            last = NE - 1
            step(v.tensor_tensor(e_re, ex_o[:, 0:NH], cos_t[:, :, last], ALU.mult))
            step(v.tensor_tensor(e_im, ex_o[:, 0:NH], sin_t[:, :, last], ALU.mult))
            step(v.tensor_scalar(e_re, e_re, 1.0, None, ALU.subtract))
            step(v.tensor_tensor(u1, a_re, a_re, ALU.mult))
            step(v.tensor_tensor(u2, a_im, a_im, ALU.mult))
            step(v.tensor_tensor(u1, u1, u2, ALU.add))
            step(v.reciprocal(den, u1))
            step(v.tensor_tensor(u1, e_re, a_re, ALU.mult))
            step(v.tensor_tensor(u2, e_im, a_im, ALU.mult))
            step(v.tensor_tensor(u1, u1, u2, ALU.add))
            step(v.tensor_tensor(w_re, u1, den, ALU.mult))
            step(v.tensor_tensor(u1, e_im, a_re, ALU.mult))
            step(v.tensor_tensor(u2, e_re, a_im, ALU.mult))
            step(v.tensor_tensor(u1, u1, u2, ALU.subtract))
            step(v.tensor_tensor(w_im, u1, den, ALU.mult))
            step(v.tensor_tensor(u1, c_re, w_re, ALU.mult))
            step(v.tensor_tensor(u2, c_im, w_im, ALU.mult))
            step(v.tensor_tensor(ct_re, u1, u2, ALU.subtract))
            step(v.tensor_tensor(u1, c_re, w_im, ALU.mult))
            step(v.tensor_tensor(u2, c_im, w_re, ALU.mult))
            step(v.tensor_tensor(ct_im, u1, u2, ALU.add))
            top, low = slice(0, NST), slice(NST, 2 * NST)
            step(v.tensor_scalar(coef_p[top], ct_re[top], 2.0, None, ALU.mult))
            step(v.tensor_scalar(coef_p[low], ct_im[low], -2.0, None, ALU.mult))
            step(v.tensor_scalar(coef_q[top], ct_im[top], -2.0, None, ALU.mult))
            step(v.tensor_scalar(coef_q[low], ct_re[low], -2.0, None, ALU.mult))
            step(v.tensor_tensor(tab1, mag_t, sin_t, ALU.mult))
            step(v.tensor_tensor(tab2, mag_t, cos_t, ALU.mult))
            step(v.tensor_tensor(g1, bc(coef_p, CA), tab2[:, :, 0:CA], ALU.mult))
            step(v.tensor_tensor(g2, bc(coef_q, CA), tab1[:, :, 0:CA], ALU.mult))
            step(v.tensor_tensor(g1, g1, g2, ALU.add))
            step(v.tensor_copy(tab1[top, :, CA:CA + CC], tab2[top, :, CA:CA + CC]), "factors")
            dve.wait_ge(s_k, 1)
            step(v.tensor_copy(ksb[0:CA].rearrange("p h c -> p (h c)"),
                               ps[0:CA, 4:6, :].rearrange("p a n -> p (a n)")))
            V_KSB[0] = n[0]

        @block.vector
        def _(dve):
            v = nc.vector
            vector_part_a(dve, v)

            def head(h, j):
                dve.wait_ge(s_y, h + 1)
                v.tensor_tensor(ym[:, j % 2, :], ps[:, j % 2, :], mask.rearrange("p k b -> p (k b)"),
                                ALU.mult).then_inc(s_ym, 1)
                dve.wait_ge(s_wh, h + 1)
                v.scalar_tensor_tensor(w_lo[:, bass.ds(h * WCH, WCH)], wring[:, j, :], S_W,
                                       w_hi[:, bass.ds(h * WCH, WCH)], ALU.mult, ALU.subtract).then_inc(s_wl, 1)
                xs = x1[:, :, bass.ds(h, 1), :].rearrange("p k a b -> p k (a b)")
                dve.wait_ge(s_ym, h + 1)
                v.tensor_tensor(xs, xs, ym[:, j % 2, :].rearrange("p (k b) -> p k b", k=KL),
                                ALU.add).then_inc(s_x1, 1)

            dve.wait_ge(s_x, 16 * (NH // HB))
            with dve.Fori(0, NH // HB) as g:
                for j in range(HB):
                    head(g * HB + j, j)
            dve.wait_ge(s_x1, NH)

            def stage_lo(t, par):
                dve.wait_ge(s_xh, t + 1)
                for k in range(KL):
                    v.scalar_tensor_tensor(xstage[:, par, 1, k].rearrange("p b h -> p h b"),
                                           x1[:, k, :, bass.ds(t * TB, TB)], S_X,
                                           xstage[:, par, 0, k].rearrange("p b h -> p h b"),
                                           ALU.mult, ALU.subtract).then_inc(s_xl, 1)

            def lora_pairs(t):
                dve.wait_ge(s_ta, t + 1)
                for b in range(4):
                    rows = slice(32 * b, 32 * b + 32)
                    v.tensor_scalar(sel[rows].rearrange("p (q g) r -> p q (g r)", q=Q),
                                    ps[rows, 7, 0:Q * P].rearrange("p (q n) -> p q n", q=Q)
                                    [:, :, 2 * R * b:2 * R * b + 2 * R],
                                    S_T / G_SCALE, None, ALU.mult).then_inc(s_sel, 1)
                dve.wait_ge(s_sel, (t + 1) * 4)
                v.tensor_copy(val[:, :, 0, :], sel[:]).then_inc(s_val, 1)
                v.tensor_copy(val[:, :, 2, :], sel[:]).then_inc(s_val, 1)
                dve.wait_ge(s_val, t * 3 + 2)
                v.scalar_tensor_tensor(val[:, :, 1, :], sel[:], 1.0, val[:, :, 0, :], ALU.mult,
                                       ALU.subtract).then_inc(s_val, 1)
                dve.wait_ge(s_val, t * 3 + 3)
                wait(dve, s_tp, t)
                for j in range(2):
                    v.tensor_scalar(tt[:, :, j, :], val[:].rearrange("p n e r -> p n (e r)"),
                                    pair_sel[:, j:j + 1], None, ALU.mult).then_inc(s_tt, 1)

            def lora_down(t):
                dve.wait_ge(s_d, (t + 1) * FT)
                wait(dve, s_t2p, t)
                for b in range(4):
                    rows = slice(32 * b, 32 * b + 32)
                    v.tensor_scalar(t2[rows, :, 2 * R * b:2 * R * b + R], ps[rows, 4:6, R * b:R * b + R],
                                    S_T2 / O_SCALE, None, ALU.mult).then_inc(s_t2h, 1)
                dve.wait_ge(s_t2h, (t + 1) * 4)
                for b in range(4):
                    rows = slice(32 * b, 32 * b + 32)
                    v.scalar_tensor_tensor(t2[rows, :, 2 * R * b + R:2 * R * (b + 1)],
                                           ps[rows, 4:6, R * b:R * b + R], S_T2 / O_SCALE,
                                           t2[rows, :, 2 * R * b:2 * R * b + R],
                                           ALU.mult, ALU.subtract).then_inc(s_t2, 1)

            def down_turned(t):
                dve.wait_ge(s_t2p, t + 1)
                wait(dve, s_acc, t)
                v.tensor_copy(t2a[:], ps[:, 6, 0:P].bitcast(F16).rearrange("p (q n) -> p q n", q=Q))\
                    .then_inc(s_t2a, 1)

            def evacuate(t):
                dve.wait_ge(s_acc, t + 1)
                wait(dve, s_out, t * 16)
                v.tensor_scalar(out_sb[:, 1, :], ps[:, 3, :], 1 / O_SCALE, None, ALU.mult).then_inc(s_ev1, 1)

            def block_act(t, par, m):
                n = t * FT + m
                turn = (par + m) % 2
                rows = slice(0, min(P, FF - m * P))
                dve.wait_ge(s_sg, n + 1)
                v.scalar_tensor_tensor(af[rows, turn], ps[rows, turn, TOK:2 * TOK], S_ACT / G_SCALE,
                                       sg[rows, turn], ALU.mult, ALU.mult).then_inc(s_af, 1)
                dve.wait_ge(s_ah, n + 1)
                v.tensor_tensor(act_hl[rows, m, 1], af[rows, turn], act_hl[rows, m, 0],
                                ALU.subtract).then_inc(s_al, 1)

            def tile(t, par, first, last):
                for m in range(FT):
                    block_act(t, par, m)
                    if m == 0 and not first:
                        lora_down(t - 1)
                    if m == 1 and not first:
                        down_turned(t - 1)
                    if m == 2 and not first:
                        evacuate(t - 1)
                    if m == 3 and not last:
                        stage_lo(t + 1, 1 - par)
                    if m == 6 and not last:
                        lora_pairs(t + 1)

            stage_lo(0, 0)
            lora_pairs(0)
            tile(0, 0, True, False)
            with dve.Fori(0, (NT - 2) // 2) as g:
                tile(g * 2 + 1, 1, False, False)
                tile(g * 2 + 2, 0, False, False)
            tile(NT - 1, 1, False, True)
            lora_down(NT - 1)
            down_turned(NT - 1)
            evacuate(NT - 1)

        @block.scalar
        def _(act):
            s = nc.scalar
            act.wait_ge(s_v, V_STEP["theta"])
            s.activation(sin_t, theta, ACT.Sin).then_inc(s_a, 1)
            act.wait_ge(s_v, V_STEP["abs_theta"])
            s.activation(cos_t, turns, ACT.Sin, bias=half_pi[:, 0:1], scale=-1.0).then_inc(s_a, 1)
            act.wait_ge(s_v, V_STEP["mag"])
            s.activation(mag_t, mag_t, ACT.Exp).then_inc(s_a, 1)

            def head(g, j, first):
                h = g * HB + j
                act.wait_ge(s_s[j], 16 * (g + 1))
                if not first:
                    act.wait_ge(s_y, h - 1)
                s.activation(toep[:, j % 2, :], s_ring[:, j, ::-1], ACT.Copy).then_inc(s_r, 1)
                act.wait_ge(s_w[j], 16 * (g + 1))
                s.activation(w_hi[:, bass.ds(h * WCH, WCH)], wring[:, j, :], ACT.Copy, scale=S_W).then_inc(s_wh, 1)

            act.wait_ge(s_k, 1)
            act.wait_ge(s_kd, 32)
            for j in range(HB):
                head(0, j, j < 2)
            with act.Fori(1, NH // HB) as g:
                for j in range(HB):
                    head(g, j, False)

            def stage_hi(t, par):
                if par == 0 and isinstance(t, int):
                    act.wait_ge(s_x1, NH)
                    act.wait_ge(s_wl, NH)
                else:
                    wait(act, s_acc, t - 1)
                s.activation(xstage[:, par, 0].rearrange("p k b h -> p k h b"),
                             x1[:, :, :, bass.ds(t * TB, TB)], ACT.Copy, scale=S_X).then_inc(s_xh, 1)

            def pairs_turned(t, par):
                act.wait_ge(s_tp, t + 1)
                wait(act, s_gu, (t - 1) * FT)
                s.activation(t_mov[0:3 * 2 * R, par].rearrange("p g q n -> p (g q n)"),
                             ps[0:3 * 2 * R, 6, 0:2 * P].bitcast(F16), ACT.Copy).then_inc(s_tm, 1)

            def evacuate(t):
                act.wait_ge(s_acc, t + 1)
                wait(act, s_out, t * 16)
                s.activation(out_sb[:, 0, :], ps[:, 2, :], ACT.Copy, scale=1 / O_SCALE).then_inc(s_ev0, 1)

            def block_act(t, par, m):
                n = t * FT + m
                turn = (par + m) % 2
                rows = slice(0, min(P, FF - m * P))
                act.wait_ge(s_gu, n + 1)
                wait(act, s_af, n - 1)
                s.activation(sg[rows, turn], ps[rows, turn, 0:TOK], ACT.Silu, scale=1 / G_SCALE).then_inc(s_sg, 1)
                act.wait_ge(s_af, n + 1)
                wait(act, s_d, n + 1 - FT)
                s.activation(act_hl[rows, m, 0], af[rows, turn], ACT.Copy).then_inc(s_ah, 1)

            def tile(t, par, first, last):
                for m in range(FT):
                    block_act(t, par, m)
                    if m == 2 and not first:
                        evacuate(t - 1)
                    if m == 3 and not last:
                        stage_hi(t + 1, 1 - par)
                    if m == 8 and not last:
                        pairs_turned(t + 1, 1 - par)

            stage_hi(0, 0)
            pairs_turned(0, 0)
            tile(0, 0, True, False)
            with act.Fori(0, (NT - 2) // 2) as g:
                tile(g * 2 + 1, 1, False, False)
                tile(g * 2 + 2, 0, False, False)
            tile(NT - 1, 1, False, True)
            evacuate(NT - 1)

        @block.tensor
        def _(pe):
            mm = nc.tensor.matmul
            pe.wait_ge(s_v, V_STEP["factors"])
            for i in range(2):
                mm(ps[0:CA, 4 + i, :], onehot, drow[0:1].rearrange("p h c -> p (h c)")[:, 512 * i:512 * i + 512],
                   start=True, stop=False, skip_group_check=True)
            for h in range(NH):
                c0 = CC * (h % 16)
                last = mm(ps[0:CA, 4 + h // 16, c0:c0 + CC], g1[:, h, :], tab1[:, h, CA:CA + CC],
                          start=False, stop=True, skip_group_check=True)
            last.then_inc(s_k, 1)

            def head(h, j, first):
                pe.wait_ge(s_r, h + 1)
                if not first:
                    pe.wait_ge(s_ym, h - 1)
                for lk in range(KL):
                    for mk in range(lk + 1):
                        last = mm(ps[:, j % 2, lk * P:(lk + 1) * P], toep[:, j % 2, (lk - mk) * P:(lk - mk + 1) * P],
                                  x1[:, mk, bass.ds(h, 1), :].rearrange("p a b -> p (a b)"),
                                  start=(mk == 0), stop=(mk == lk))
                last.then_inc(s_y, 1)

            pe.wait_ge(s_x, 16 * (NH // HB))
            for j in range(HB):
                head(j, j, j < 2)
            with pe.Fori(1, NH // HB) as g:
                for j in range(HB):
                    head(g * HB + j, j, False)

            def lora_a(t, par):
                pe.wait_ge(s_xl, (t + 1) * KL)
                pe.wait_ge(s_ga, 16 * TB * (t + 1))
                wait(pe, s_tt, t * 2)
                if isinstance(t, int) and t == 0:
                    pe.wait_ge(s_wl, NH)
                for q in range(Q):
                    for k in range(KL):
                        for xe, ae in ((0, 0), (0, 1), (1, 0)):
                            last = mm(ps[:, 7, q * P:(q + 1) * P],
                                      xstage[:, par, xe, k, 4 * q:4 * q + 4, :].rearrange("p b h -> p (b h)"),
                                      a_buf[:, 4 * q:4 * q + 4, ae, k, :],
                                      start=(k == 0 and xe == 0 and ae == 0), stop=(k == KL - 1 and xe == 1))
                last.then_inc(s_ta, 1)

            def turn_pairs(t):
                pe.wait_ge(s_tt, (t + 1) * 2)
                wait(pe, s_t2a, t - 1)
                for g in range(2):
                    for q in range(Q):
                        last = nc.tensor.transpose(ps[0:3 * 2 * R, 6, (g * Q + q) * 64:(g * Q + q) * 64 + 64].bitcast(F16),
                                                   tt[:, q * 2 + g].rearrange("p j n -> p (j n)"), ident[:])
                last.then_inc(s_tp, 1)

            def gate_up(t, par, m):
                n = t * FT + m
                turn = (par + m) % 2
                f = min(P, FF - m * P)
                wait(pe, s_af, n - 1)
                if m == 0:
                    pe.wait_ge(s_tm, t + 1)
                if m * P == 0:
                    pe.wait_ge(s_gb[0], 16 * TB * (t + 1))
                if m * P == FH0:
                    pe.wait_ge(s_gb[1], 16 * TB * (t + 1))
                half = 1 if m * P >= FH0 else 0
                fo = m * P - half * FH0
                for g in range(2):
                    o = ps[0:f, turn, g * TOK:(g + 1) * TOK]
                    for k in range(KL):
                        c0 = (g * KL + k) * FF + m * P
                        for we, xe in ((0, 0), (0, 1), (1, 0)):
                            w = (w_hi, w_lo)[we]
                            mm(o, w[:, c0:c0 + f], xstage[:, par, xe, k].rearrange("p b h -> p (b h)"),
                               start=(k == 0 and we == 0 and xe == 0), stop=False)
                    for j in range(4):
                        last = mm(ps[0:f, turn, g * TOK + 64 * j:g * TOK + 64 * j + 64],
                                  b_half[half][0:3 * 2 * R, j, g, fo:fo + f],
                                  t_mov[0:3 * 2 * R, par, g, j // 2, 64 * (j % 2):64 * (j % 2) + 64],
                                  start=False, stop=(j == 3))
                last.then_inc(s_gu, 1)

            def down(t, m):
                kf = min(P, FF - m * P)
                pe.wait_ge(s_al, t * FT + m + 1)
                if m == 0:
                    pe.wait_ge(s_gad, 16 * TB * (t + 1))
                    wait(pe, s_ev0, t)
                    wait(pe, s_ev1, t)
                    wait(pe, s_t2, t * 4)
                for q in range(Q):
                    w = slice(WD0 + m * NL, WD0 + (m + 1) * NL)
                    for ae, we in ((0, 0), (0, 1), (1, 0)):
                        a = act_hl[0:kf, m, ae, q * P:(q + 1) * P]
                        first = m == 0 and ae == 0 and we == 0
                        mm(ps[:, 2 + q, :], a, (w_hi, w_lo)[we][0:kf, w], start=first, stop=False)
                        last = mm(ps[:, 4 + q, 0:4 * R], a, ad_buf[0:kf, 4 * q:4 * q + 4, we, m, :],
                                  start=first, stop=(m == FT - 1 and ae == 1))
                last.then_inc(s_d, 1)

            def turn_down(t):
                pe.wait_ge(s_t2, (t + 1) * 4)
                wait(pe, s_tm, t + 1)
                for q in range(Q):
                    last = nc.tensor.transpose(ps[:, 6, q * 64:q * 64 + 64].bitcast(F16), t2[:, q, :], ident[:])
                last.then_inc(s_t2p, 1)

            def finish(t, par):
                pe.wait_ge(s_t2a, t + 1)
                pe.wait_ge(s_gbd, 16 * TB * (t + 1))
                for q in range(Q):
                    for e in range(2):
                        mm(ps[:, 2 + q, :], t2a[:, q, :], bd_buf[:, q, e, :], start=False, stop=False)
                    for k in range(KL):
                        for e in range(2):
                            last = mm(ps[:, 2 + q, k * P:(k + 1) * P], xstage[:, par, e, k, 4 * q:4 * q + 4, :].rearrange("p b h -> p (b h)"),
                                      ident_x[:], start=False, stop=(k == KL - 1 and e == 1))
                last.then_inc(s_acc, 1)

            def tile(t, par, first, last):
                for m in range(FT):
                    gate_up(t, par, m)
                    if not first:
                        if m == 0:
                            down(t - 1, FT - 1)
                        if m == 1:
                            turn_down(t - 1)
                        if m == 2:
                            finish(t - 1, 1 - par)
                    if m == 6 and not last:
                        lora_a(t + 1, 1 - par)
                    if m == 8 and not last:
                        turn_pairs(t + 1)
                    for d in DOWN_AT.get(m, ()):
                        down(t, d)

            DOWN_AT = {4: (0, 1, 2), 5: (3, 4), 6: (5,), 7: (6,), 8: (7,), 9: (8,), 10: (9,)}
            lora_a(0, 0)
            turn_pairs(0)
            tile(0, 0, True, False)
            with pe.Fori(0, (NT - 2) // 2) as g:
                tile(g * 2 + 1, 1, False, False)
                tile(g * 2 + 2, 0, False, False)
            tile(NT - 1, 1, False, True)
            down(NT - 1, FT - 1)
            turn_down(NT - 1)
            finish(NT - 1, 1)

        @block.sync
        def _(sp):
            sp.dma_start(ex_in[:, 0:NH], ldt.partition_broadcast(P)).then_inc(s_par, 16)
            for i in range(2):
                h = slice(NST * i, NST * (i + 1))
                sp.dma_start(ex_in[h, NH:2 * NH], lar).then_inc(s_par, 16)
                sp.dma_start(a_im[h, :], aim).then_inc(s_par, 16)
                sp.dma_start(c_re[h, :], cst[0]).then_inc(s_par, 16)
                sp.dma_start(c_im[h, :], cst[1]).then_inc(s_par, 16)
            sp.dma_start(leni, length.partition_broadcast(P)).then_inc(s_par, 16)
            sp.dma_start(dval, dvec.unsqueeze(0)).then_inc(s_par, 16)
            for g in range(NH // HB):
                sp.dma_start(x1[:, :, g * HB:(g + 1) * HB, :],
                             xt[:, g].rearrange("p k (h b) -> p k h b", h=HB)).then_inc(s_x, 16)
            sp.wait_ge(s_pool, 1)
            sp.dma_start(krev[:, NL:KROW], zrow).then_inc(s_kd, 16)
            sp.wait_ge(s_v, V_KSB[0])
            sp.dma_start(krev[:, 0:NL].rearrange("h (a c) -> a h c", a=CA), ksb[0:CA]).then_inc(s_kd, 16)
            sp.wait_ge(s_kd, 32)

            def head_loads(h, slot, first):
                if not first:
                    sp.wait_ge(s_r, h - HB + 1)
                sp.dma_start(s_ring[:, slot, :], strip(h)).then_inc(s_s[slot], 16)
                if not first:
                    sp.wait_ge(s_wl, h - HB + 1)
                sp.dma_start(wring[:, slot, :], wall[:, bass.ds(h * WCH, WCH)]).then_inc(s_w[slot], 16)

            def strip(h):
                return bass.AP(krev.tensor, h * KROW, [[1, P], [1, NL]])

            for j in range(HB):
                head_loads(j, j, True)
            with sp.Fori(1, NH // HB) as g:
                for j in range(HB):
                    head_loads(g * HB + j, j, False)

            for i in range(2):
                sp.wait_ge(s_lo[i], 16 * STORES[len(LPARTS) - 2 + i])

            def indices(t):
                return [sp.value_load(adapter[:, bass.ds(t * TB + j, 1)], min_val=0, max_val=NAD - 1)
                        for j in range(TB)]

            def fetch_a(t):
                idx = indices(t)
                wait(sp, s_ta, t)
                for j, a in enumerate(idx):
                    sp.dma_start(a_buf[:, j].rearrange("p e k n -> p e (k n)"),
                                 a_scr[bass.ds(a, 1)].squeeze(0)).then_inc(s_ga, 16)

            def fetch_rest(t, prev):
                idx = indices(t)
                for half in range(2):
                    if prev:
                        sp.wait_ge(s_gu, (t - 1) * FT + (FH0 // P if half == 0 else FT))
                    f0 = FH0 * half
                    for j, a in enumerate(idx):
                        r0 = 3 * R * (j % 2)
                        sp.dma_start(b_half[half][r0:r0 + 3 * R, j // 2],
                                     b_scr[bass.ds(a, 1), :, :, :, f0:f0 + FHS[half]]
                                     .rearrange("a e r g f -> (a e r) g f")).then_inc(s_gb[half], 16)
                if prev:
                    sp.wait_ge(s_d, t * FT)
                for j, a in enumerate(idx):
                    sp.dma_start(ad_buf[:, j].rearrange("p e k n -> p e (k n)"),
                                 ad_scr[bass.ds(a, 1)].squeeze(0)).then_inc(s_gad, 16)
                if prev:
                    sp.wait_ge(s_acc, t)
                for j, a in enumerate(idx):
                    r0 = 2 * R * (j % 4)
                    sp.dma_start(bd_buf[r0:r0 + 2 * R, j // 4],
                                 bd_scr[bass.ds(a, 1)].rearrange("a e r g f -> (a e r) g f")).then_inc(s_gbd, 16)

            def store(t):
                sp.wait_ge(s_ev0, t + 1)
                sp.wait_ge(s_ev1, t + 1)
                sp.dma_start(out[bass.ds(t * TOK, TOK), :].rearrange("(q p) n -> p q n", q=Q), out_sb[:])\
                    .then_inc(s_out, 16)

            fetch_a(0)
            fetch_rest(0, False)
            fetch_a(1)
            fetch_rest(1, True)
            with sp.Fori(2, NT) as t:
                store(t - 2)
                fetch_a(t)
                fetch_rest(t, True)
            store(NT - 2)
            store(NT - 1)
            sp.wait_ge(s_out, 16 * NT)

        @block.gpsimd
        def _(pool):
            g = nc.gpsimd
            g.memset(zrow, 0.0).then_inc(s_pool, 1)
            g.iota(lags[:, 0:CA], [[-CC, CA]], base=CC * (CA - 1), channel_multiplier=0,
                   allow_small_or_imprecise_dtypes=True).then_inc(s_pool, 1)
            g.iota(lags[:, CA:CA + CC], [[-1, CC]], base=CC - 1, channel_multiplier=0,
                   allow_small_or_imprecise_dtypes=True).then_inc(s_pool, 1)
            g.memset(lags[:, CA + CC:NE], 1.0).then_inc(s_pool, 1)
            g.iota(ioti.rearrange("p (k b) -> p k b", k=KL), [[P, KL], [0, NB]], base=0, channel_multiplier=1,
                   allow_small_or_imprecise_dtypes=True).then_inc(s_pool, 1)
            g.memset(onehot, 0.0).then_inc(s_pool, 1)
            g.memset(ident[:], 0.0).then_inc(s_pool, 1)
            g.memset(ident_x[:], 0.0).then_inc(s_pool, 1)
            pool.wait_ge(s_pool, 8)
            g.memset(onehot[:, CA - 1:CA], 1.0).then_inc(s_pool, 1)
            for m, v in ((ident, 1.0), (ident_x, O_SCALE / S_X)):
                g.affine_select(out=m[:], in_=m[:], compare_op=ALU.not_equal, fill=v, base=0,
                                pattern=[[-1, P]], channel_multiplier=1).then_inc(s_pool, 1)
            g.memset(half_pi[:], TWO_PI / 4).then_inc(s_pool, 1)

            off = [sum(n for _, _, n in LPARTS[:i]) for i in range(len(LPARTS))]

            def load(i):
                if i >= 2:
                    pool.wait_ge(s_lc, 3 * (i - 1))
                n = LPARTS[i][2]
                pool.dma_start(lora_in[i % 2][:, 0:n], lora[:, off[i]:off[i] + n]).then_inc(s_li[i % 2], 16)

            load(0)
            load(1)
            for i, (kind, part, n) in enumerate(LPARTS):
                v, hi, lo = lora_in[i % 2][:, 0:n], lora_hi[i % 2][:, 0:n], lora_lo[i % 2][:, 0:n]
                pool.wait_ge(s_li[i % 2], 16 * (i // 2 + 1))
                g.tensor_scalar(v, v, S_W, None, ALU.mult).then_inc(s_lc, 1)
                if i >= 2:
                    pool.wait_ge(s_lo[i % 2], 16 * STORES[i - 2])
                pool.wait_ge(s_lc, 3 * i + 1)
                g.tensor_copy(hi, v).then_inc(s_lc, 1)
                pool.wait_ge(s_lc, 3 * i + 2)
                g.tensor_tensor(lo, v, hi, ALU.subtract).then_inc(s_lc, 1)
                if i + 2 < len(LPARTS):
                    load(i + 2)
                pool.wait_ge(s_lc, 3 * i + 3)
                if kind == "A":
                    a0 = part * (NAD // 2)
                    for e, src in enumerate((hi, lo)):
                        pool.dma_start(a_scr[a0:a0 + NAD // 2, :, e, :].rearrange("a p n -> p a n"),
                                       src.rearrange("p (a n) -> p a n", a=NAD // 2)).then_inc(s_lo[i % 2], 16)
                elif kind == "B":
                    blk, gu = part
                    for e, src in enumerate((hi, hi, lo)):
                        for_a = b_scr[8 * blk:8 * blk + 8, e, :, gu, :]
                        pool.dma_start(for_a, src).then_inc(s_lo[i % 2], 16)
                elif kind == "Ad":
                    for e, src in enumerate((hi, lo)):
                        pool.dma_start(ad_scr[4 * part:4 * part + 4, :, e, :].rearrange("a p n -> p a n"),
                                       src.rearrange("p (a n) -> p a n", a=4)).then_inc(s_lo[i % 2], 16)
                else:
                    for d in range(2):
                        for e, src in enumerate((hi, lo)):
                            pool.dma_start(bd_scr[8 * part:8 * part + 8, d, :, e, :], src).then_inc(s_lo[i % 2], 16)


def kernel(x, itok_B_78_3631, itok_B_2_6, L0_cond_log_dt, L0_cond_C, L0_cond_log_A_real, L0_cond_A_imag, L0_cond_D,
           L1_cond_W_gate, L1_cond_W_up, L1_cond_W_down, L1_cond_A_gate, L1_cond_B_gate, L1_cond_A_up,
           L1_cond_B_up, L1_cond_A_down, L1_cond_B_down):
    import numpy as np
    import concourse.bacc as bacc
    from concourse.bass_utils import run_bass_kernel_spmd

    def arr(a):
        return np.asarray(a)

    xt = arr(x).transpose(2, 1, 0).reshape(KL, P, NH // 4, 4 * NB).transpose(1, 2, 0, 3)
    wall = np.zeros((P, NW), np.float32)
    for g, w in enumerate((L1_cond_W_gate, L1_cond_W_up)):
        wall[:, g * KL * FF:(g + 1) * KL * FF] = arr(w).T.reshape(KL, P, FF).transpose(1, 0, 2).reshape(P, KL * FF)
    wd = np.zeros((FT * P, NL), np.float32)
    wd[:FF] = arr(L1_cond_W_down).T
    wall[:, WD0:] = wd.reshape(FT, P, NL).transpose(1, 0, 2).reshape(P, FT * NL)
    a_gu = np.stack([arr(L1_cond_A_gate)[0], arr(L1_cond_A_up)[0]])
    a_gu = a_gu.reshape(2, NAD, R, KL, P).transpose(4, 1, 3, 0, 2).reshape(P, 2, NLA)
    parts = [a_gu[:, 0], a_gu[:, 1]]
    b_t = [arr(b)[0].transpose(0, 2, 1).reshape(NAD * R, FF) for b in (L1_cond_B_gate, L1_cond_B_up)]
    parts += [b_t[gu][blk * P:(blk + 1) * P] for blk in range(2) for gu in range(2)]
    ad = np.zeros((NAD, R, FT * P), np.float32)
    ad[:, :, :FF] = arr(L1_cond_A_down)[0]
    ad = ad.reshape(NAD, R, FT, P).transpose(3, 0, 2, 1).reshape(P, 4, 4 * FT * R)
    parts += [ad[:, g] for g in range(4)]
    bd = arr(L1_cond_B_down)[0].transpose(0, 2, 1).reshape(NAD * R, NL)
    parts += [bd[:P], bd[P:]]
    ins = {
        "xt": xt, "wall": wall, "lora": np.concatenate(parts, axis=1),
        "ldt": arr(L0_cond_log_dt), "lar": arr(L0_cond_log_A_real).T, "aim": arr(L0_cond_A_imag).T,
        "cst": arr(L0_cond_C).transpose(2, 1, 0), "dvec": arr(L0_cond_D),
        "length": arr(itok_B_78_3631), "adapter": arr(itok_B_2_6).reshape(1, NB),
    }
    nc = bacc.Bacc("TRN2", target_bir_lowering=False, num_devices=1)
    arrays, aps = {}, {}
    for name, a in ins.items():
        a = np.ascontiguousarray(a)
        arrays[name] = a
        aps[name] = nc.dram_tensor(name, a.shape, mybir.dt.from_np(a.dtype), kind="ExternalInput").ap()
    y = nc.dram_tensor("y", (NB * NH, NL), F32, kind="ExternalOutput").ap()
    build(nc, out=y, **aps)
    r = run_bass_kernel_spmd(nc, [arrays], core_ids=[0])
    return r.results[0]["y"].reshape(NB, NH, NL)
```

```python
from contextlib import ExitStack

import concourse.bass as bass
from concourse import mybir

F32 = mybir.dt.float32
F16 = mybir.dt.float16
I32 = mybir.dt.int32
ALU = mybir.AluOpType
ACT = mybir.ActivationFunctionType

P = 128
NB, NH, NL = 128, 32, 512
NST = 64
FF = 1376
R = 16
NAD = 16
KL = NL // P
FT = (FF + P - 1) // P
FLAST = FF - (FT - 1) * P
FH0 = 6 * P
FH1 = FF - FH0
FHS = [FH0, FH1]
CA, CC = 16, 32
KROW = NL + P
NW = 2 * KL * FF + FT * NL
WD0 = 2 * KL * FF
WCH = NW // NH
TB = 8
NT = NB // TB
TOK = TB * NH
Q = TOK // P
assert NW % NH == 0

S_X, S_W, S_T, S_ACT, S_T2 = 8.0, 256.0, 4.0, 4.0, 2.0
G_SCALE = S_X * S_W
O_SCALE = S_ACT * S_W
assert S_T * S_W == 0.5 * G_SCALE and S_T2 * S_W == 0.5 * O_SCALE

TWO_PI = 6.283185307179586
PI_HI = 6.28125
PI_LO = TWO_PI - PI_HI
LN2 = 0.6931471805599453
LN2_HI = 0.693145751953125
LN2_LO = LN2 - LN2_HI
MAGIC = 12582912.0
EXP_C = [1 / 5040, 1 / 720, 1 / 120, 1 / 24, 1 / 6, 0.5, 1.0, 1.0]

NLA = 2 * KL * R * NAD // 2
LPARTS = [("A", h, NLA) for h in range(2)]
LPARTS += [("B", (blk, gu), FF) for blk in range(2) for gu in range(2)]
LPARTS += [("Ad", g, 4 * FT * R) for g in range(4)]
LPARTS += [("Bd", blk, NL) for blk in range(2)]
NLO = sum(n for _, _, n in LPARTS)


def build(nc, xt, wall, lora, par, dvec, length, adapter, out):
    ctx = ExitStack()
    with ctx:
        def sb(name, shape, dt):
            return ctx.enter_context(nc.sbuf_tensor(name, shape, dt))

        def sem(name):
            return ctx.enter_context(nc.semaphore(name))

        krev = nc.dram_tensor("krev", [NH, KROW], F32, kind="Internal").ap()
        a_scr = nc.dram_tensor("a_scr", [NAD, P, 2, 2 * KL * R], F16, kind="Internal").ap()
        b_scr = nc.dram_tensor("b_scr", [NAD, 3, R, 2, FF], F16, kind="Internal").ap()
        ad_scr = nc.dram_tensor("ad_scr", [NAD, P, 2, FT * R], F16, kind="Internal").ap()
        bd_scr = nc.dram_tensor("bd_scr", [NAD, 2, R, 2, NL], F16, kind="Internal").ap()

        w_hi = sb("w_hi", [P, NW], F16)
        w_lo = sb("w_lo", [P, NW], F16)
        x1 = sb("x1", [P, KL, NH, NB], F32)
        up_lora = sb("up_lora", [P, 4 * 2 * FF], F16)
        lora_in = [up_lora[:, 4 * FF * i:4 * FF * i + 2 * FF].bitcast(F32) for i in range(2)]
        lora_hi = [up_lora[:, 4 * FF * i + 2 * FF:4 * FF * i + 3 * FF] for i in range(2)]
        lora_lo = [up_lora[:, 4 * FF * i + 3 * FF:4 * FF * i + 4 * FF] for i in range(2)]
        b_half = [up_lora[:, 0:8 * FH0].rearrange("p (j g f) -> p j g f", j=4, g=2),
                  up_lora[:, 8 * FH0:8 * FF].rearrange("p (j g f) -> p j g f", j=4, g=2)]
        a_buf = sb("a_buf", [P, TB, 2, KL, 2 * R], F16)
        ad_buf = sb("ad_buf", [P, TB, 2, FT, R], F16)
        down_lora = sb("down_lora", [P, 2 * FT * R * TB], F16)
        bd_buf = down_lora[:, 0:Q * 2 * NL].rearrange("p (q e n) -> p q e n", q=Q, e=2)
        xstage = sb("xstage", [P, 2, 2, KL, TB, NH], F16)
        wring = sb("wring", [P, 4, WCH], F32)
        act_hl = sb("act_hl", [P, FT, 2, TOK], F16)
        s_ring = act_hl[:, :, :, :].rearrange("p m e t -> p (m e t)")[:, 0:4 * 2 * NL].bitcast(F32)\
            .rearrange("p (s n) -> p s n", s=4)
        toep = xstage[:, 0].rearrange("p e k b h -> p (e k b h)").bitcast(F32).rearrange("p (s n) -> p s n", s=2)
        t_mov = sb("t_mov", [P, 2, 2, Q, P], F16)
        sg = sb("sg", [P, 2, TOK], F32)
        af = sb("af", [P, 2, TOK], F32)
        out_sb = sb("out_sb", [P, Q, NL], F32)
        mask = sg[:].rearrange("p a n -> p (a n)").rearrange("p (k b) -> p k b", k=KL)
        ym = out_sb
        sel = sb("sel", [P, Q * 2, R], F32)
        val = sb("val", [P, Q * 2, 3, R], F16)
        tt = sb("tt", [P, Q * 2, 2, 3 * R], F16)
        t2 = sb("t2", [P, Q, P], F16)
        t2a = sb("t2a", [P, Q, P], F16)
        ident = sb("ident", [P, P], F16)
        ident_x = sb("ident_x", [P, P], F16)
        pair_sel = sb("pair_sel", [P, 2], F32)
        half_pi = sb("half_pi", [P, 1], F32)
        adapter_sb = sb("adapter_sb", [1, NB], I32)

        wf = [w_hi[:, :].bitcast(F32), w_lo[:, :].bitcast(F32)]
        NE = CA + CC + 1
        NX = NH * NE

        def tmp(i, n0, shape):
            n = 1
            for s in shape:
                n *= s
            v = wf[i][:, n0:n0 + n]
            if len(shape) == 2:
                v = v.rearrange("p (a b) -> p a b", a=shape[0])
            return v

        theta = tmp(0, 0, [NH, NE])
        turns = tmp(0, NX, [NH, NE])
        sin_t = tmp(0, 2 * NX, [NH, NE])
        cos_t = tmp(0, 3 * NX, [NH, NE])
        mag_t = tmp(0, 4 * NX, [NH, NE])
        FAC1, STEP, FAC2 = slice(0, CA), CA, slice(CA + 1, NE)
        abs_t = tmp(1, 0, [NH, NE])
        fac2 = tmp(1, NX, [NH, CC])
        g1 = tmp(1, 2 * NX, [NH, CA])
        g2 = tmp(1, 2 * NX + NH * CA, [NH, CA])
        drow = tmp(1, 2 * NX + 2 * NH * CA, [NH, CC])
        ksb = tmp(1, 2 * NX + 2 * NH * CA + NH * CC, [NH, CC])
        at1 = 2 * NX + 2 * NH * CA + 2 * NH * CC
        lags = wf[1][:, at1:at1 + NE]
        ioti = wf[1][:, at1 + 64:at1 + 64 + KL * NB]
        leni = wf[1][:, at1 + 64 + KL * NB:at1 + 64 + KL * NB + NB].bitcast(I32)
        lenf = wf[1][:, at1 + 64 + KL * NB + NB:at1 + 64 + KL * NB + 2 * NB]
        at1 += 64 + KL * NB + 2 * NB
        zrow = wf[1][0:NH, at1:at1 + P]
        onehot = wf[1][0:1, at1 + P:at1 + P + CA]
        dval = wf[1][0:1, at1 + P + CA:at1 + P + CA + NH]
        small0 = at1 + P + CA + NH
        s0 = [0]

        def col(n=NH):
            s0[0] += n
            assert small0 + s0[0] <= NW // 2
            return wf[1][:, small0 + s0[0] - n:small0 + s0[0]]
        params = col(5 * NH)
        ex_in = params[:, 0:2 * NH]
        a_im, c_re, c_im = [params[:, i * NH:(i + 1) * NH] for i in (2, 3, 4)]
        ex_k, ex_r, ex_p, ex_o = [col(2 * NH) for _ in range(4)]
        a_re, d_re, d_im, e_re, e_im, w_re, w_im, den, ct_re, ct_im, u1, u2, coef_p, coef_q = \
            [col() for _ in range(14)]

        ps = ctx.enter_context(nc.psum_tensor("ps", [P, 8, 512], F32))

        s_par = sem("s_par")
        s_x = sem("s_x")
        s_pool = sem("s_pool")
        s_v = sem("s_v")
        s_a = sem("s_a")
        s_k = sem("s_k")
        s_kd = sem("s_kd")
        assert FT % 2 == 1
        HB = 4
        s_s = [sem(f"s_s{i}") for i in range(HB)]
        s_r = sem("s_r")
        s_w = [sem(f"s_w{i}") for i in range(HB)]
        s_y = sem("s_y")
        s_ym = sem("s_ym")
        s_x1 = sem("s_x1")
        s_wh = sem("s_wh")
        s_wl = sem("s_wl")
        s_li = [sem(f"s_li{i}") for i in range(2)]
        s_lc = sem("s_lc")
        s_lh = sem("s_lh")
        s_mag = sem("s_mag")
        s_lo2 = [sem(f"s_lo2{i}") for i in range(2)]
        s_lo = [sem(f"s_lo{i}") for i in range(2)]
        s_ga = sem("s_ga")
        s_gb = [sem(f"s_gb{i}") for i in range(2)]
        s_gad = sem("s_gad")
        s_gbd = sem("s_gbd")
        s_xh = sem("s_xh")
        s_xl = sem("s_xl")
        s_ta = sem("s_ta")
        s_tt = sem("s_tt")
        s_tp = sem("s_tp")
        s_tm = sem("s_tm")
        s_sel = sem("s_sel")
        s_val = sem("s_val")
        s_t2h = sem("s_t2h")
        s_gu = sem("s_gu")
        s_sg = sem("s_sg")
        s_af = sem("s_af")
        s_ah = sem("s_ah")
        s_al = sem("s_al")
        s_d = sem("s_d")
        s_t2 = sem("s_t2")
        s_t2p = sem("s_t2p")
        s_t2a = sem("s_t2a")
        s_acc = sem("s_acc")
        s_ev0 = sem("s_ev0")
        s_ev1 = sem("s_ev1")
        s_out = sem("s_out")

        def wait(eng, s, v):
            if not isinstance(v, int) or v > 0:
                eng.wait_ge(s, v)

        block = ctx.enter_context(nc.Block())
        NPAR = 4

        N_STORE = {"A": 2, "B": 3, "Ad": 2, "Bd": 4}
        N_FIRST = sum(kind in ("A", "B") for kind, _, _ in LPARTS)
        STORES, LC = [], []
        for i, (kind, _, _) in enumerate(LPARTS):
            STORES.append((STORES[i - 2] if i >= 2 and i != N_FIRST and i != N_FIRST + 1 else 0) + N_STORE[kind])
            LC.append((LC[-1] if i else 0) + (1 if i < N_FIRST else 3))
        OFF = [sum(n for _, _, n in LPARTS[:i]) for i in range(len(LPARTS))]

        def store_sem(i):
            return (s_lo if i < N_FIRST else s_lo2)[i % 2]

        def piece(i):
            n = LPARTS[i][2]
            if i >= N_FIRST:
                flat = down_lora[:, :] if i % 2 else ad_buf[:].rearrange("p b e k r -> p (b e k r)")
                return flat[:, 0:2 * n].bitcast(F32), flat[:, 2 * n:3 * n], flat[:, 3 * n:4 * n]
            return lora_in[i % 2][:, 0:n], lora_hi[i % 2][:, 0:n], lora_lo[i % 2][:, 0:n]

        def load_piece(pool, i):
            if i >= 2:
                pool.wait_ge(s_lc, LC[i - 2])
            pool.dma_start(piece(i)[0], lora[:, OFF[i]:OFF[i] + LPARTS[i][2]]).then_inc(s_li[i % 2], 16)

        V_STEP = {}
        V_KSB = [0]

        def vector_part_a(dve, v):
            n = [0]

            def step(ins, name=None):
                n[0] += 1
                ins.then_inc(s_v, 1)
                dve.wait_ge(s_v, n[0])
                if name:
                    V_STEP[name] = n[0]

            def exp_poly(x, k, r, p, o):
                step(v.tensor_scalar(k, x, 1 / LN2, -125.0, ALU.mult, ALU.max))
                step(v.tensor_scalar(k, k, 126.0, MAGIC, ALU.min, ALU.add))
                step(v.tensor_scalar(k, k, MAGIC, None, ALU.subtract))
                step(v.scalar_tensor_tensor(r, k, -LN2_HI, x, ALU.mult, ALU.add))
                step(v.scalar_tensor_tensor(r, k, -LN2_LO, r, ALU.mult, ALU.add))
                step(v.tensor_scalar(p, r, EXP_C[0], None, ALU.mult))
                for c in EXP_C[1:-1]:
                    step(v.scalar_tensor_tensor(p, p, c, r, ALU.add, ALU.mult))
                step(v.tensor_scalar(o.bitcast(I32), k, 127.0, 8388608.0, ALU.add, ALU.mult))
                step(v.scalar_tensor_tensor(o, p, 1.0, o, ALU.add, ALU.mult))

            def bc(x, m):
                return x.unsqueeze(2).to_broadcast([x.shape[0], NH, m])

            dve.wait_ge(s_par, 16 * NPAR)
            exp_poly(ex_in, ex_k, ex_r, ex_p, ex_o)
            dt = ex_o[:, 0:NH]
            step(v.tensor_scalar(a_re, ex_o[:, NH:2 * NH], -1.0, None, ALU.mult))
            step(v.tensor_tensor(d_re, a_re, dt, ALU.mult), "d_re")
            step(v.tensor_tensor(d_im, a_im, dt, ALU.mult))
            dve.wait_ge(s_pool, 14)
            lagb = lags.unsqueeze(1).to_broadcast([P, NH, NE])
            step(v.tensor_tensor(theta, bc(d_im, NE), lagb, ALU.mult))
            step(v.tensor_scalar(turns, theta, 1 / TWO_PI, MAGIC, ALU.mult, ALU.add))
            step(v.tensor_scalar(turns, turns, MAGIC, None, ALU.subtract))
            step(v.scalar_tensor_tensor(theta, turns, -PI_HI, theta, ALU.mult, ALU.add))
            step(v.scalar_tensor_tensor(theta, turns, -PI_LO, theta, ALU.mult, ALU.add))
            step(v.tensor_scalar(theta, theta, 3.1415925, -3.1415925, ALU.min, ALU.max), "theta")
            step(v.scalar_tensor_tensor(abs_t, theta, -1.0, theta, ALU.mult, ALU.max), "abs_theta")
            step(v.tensor_tensor(u1, a_re, a_re, ALU.mult))
            step(v.tensor_tensor(u2, a_im, a_im, ALU.mult))
            step(v.tensor_tensor(u1, u1, u2, ALU.add))
            step(v.reciprocal(den, u1))
            exp_poly(d_re, ex_k[:, 0:NH], ex_r[:, 0:NH], ex_p[:, 0:NH], ex_o[:, 0:NH])
            dve.wait_ge(s_a, 4)
            step(v.tensor_tensor(e_re, ex_o[:, 0:NH], cos_t[:, :, STEP], ALU.mult))
            step(v.tensor_tensor(e_im, ex_o[:, 0:NH], sin_t[:, :, STEP], ALU.mult))
            step(v.tensor_scalar(e_re, e_re, 1.0, None, ALU.subtract))
            step(v.tensor_tensor(u1, e_re, a_re, ALU.mult))
            step(v.tensor_tensor(u2, e_im, a_im, ALU.mult))
            step(v.tensor_tensor(u1, u1, u2, ALU.add))
            step(v.tensor_tensor(w_re, u1, den, ALU.mult))
            step(v.tensor_tensor(u1, e_im, a_re, ALU.mult))
            step(v.tensor_tensor(u2, e_re, a_im, ALU.mult))
            step(v.tensor_tensor(u1, u1, u2, ALU.subtract))
            step(v.tensor_tensor(w_im, u1, den, ALU.mult))
            step(v.tensor_tensor(u1, c_re, w_re, ALU.mult))
            step(v.tensor_tensor(u2, c_im, w_im, ALU.mult))
            step(v.tensor_tensor(ct_re, u1, u2, ALU.subtract))
            step(v.tensor_tensor(u1, c_re, w_im, ALU.mult))
            step(v.tensor_tensor(u2, c_im, w_re, ALU.mult))
            step(v.tensor_tensor(ct_im, u1, u2, ALU.add))
            top, low = slice(0, NST), slice(NST, 2 * NST)
            step(v.tensor_scalar(coef_p[top], ct_re[top], 2.0, None, ALU.mult))
            step(v.tensor_scalar(coef_p[low], ct_im[low], -2.0, None, ALU.mult))
            step(v.tensor_scalar(coef_q[top], ct_im[top], -2.0, None, ALU.mult))
            step(v.tensor_scalar(coef_q[low], ct_re[low], -2.0, None, ALU.mult))
            step(v.tensor_tensor(g1, bc(coef_p, CA), cos_t[:, :, FAC1], ALU.mult))
            step(v.tensor_tensor(g2, bc(coef_q, CA), sin_t[:, :, FAC1], ALU.mult))
            step(v.tensor_tensor(g1, g1, g2, ALU.add))
            step(v.tensor_tensor(g1, g1, mag_t[:, :, FAC1], ALU.mult))
            dve.wait_ge(s_a, 5)
            step(v.tensor_tensor(fac2, mag_t[:, :, FAC2], sin_t[:, :, FAC2], ALU.mult), "factors")
            step(v.tensor_copy(drow[0:1, :, CC - 1], dval), "drow")
            step(v.tensor_copy(lenf, leni))
            step(v.tensor_tensor(mask, lenf.unsqueeze(1).to_broadcast([P, KL, NB]),
                                 ioti.rearrange("p (k b) -> p k b", k=KL), ALU.is_gt))
            step(v.memset(pair_sel[:], 0.0))
            for b in range(4):
                step(v.memset(pair_sel[32 * b:32 * b + 32, b % 2:b % 2 + 1], 1.0))
            dve.wait_ge(s_k, 1)
            step(v.tensor_copy(ksb[0:CA].rearrange("p h c -> p (h c)"),
                               ps[0:CA, 4:6, :].rearrange("p a n -> p (a n)")))
            V_KSB[0] = n[0]

        @block.vector
        def _(dve):
            v = nc.vector
            vector_part_a(dve, v)

            def head(h, j):
                dve.wait_ge(s_y, h + 1)
                v.tensor_tensor(ym[:, j % 2, :], ps[:, j % 2, :], mask.rearrange("p k b -> p (k b)"),
                                ALU.mult).then_inc(s_ym, 1)
                dve.wait_ge(s_wh, h + 1)
                v.scalar_tensor_tensor(w_lo[:, bass.ds(h * WCH, WCH)], wring[:, j, :], S_W,
                                       w_hi[:, bass.ds(h * WCH, WCH)], ALU.mult, ALU.subtract).then_inc(s_wl, 1)
                xs = x1[:, :, bass.ds(h, 1), :].rearrange("p k a b -> p k (a b)")
                dve.wait_ge(s_ym, h + 1)
                v.tensor_tensor(xs, xs, ym[:, j % 2, :].rearrange("p (k b) -> p k b", k=KL),
                                ALU.add).then_inc(s_x1, 1)

            dve.wait_ge(s_x, 16 * (NH // HB))
            with dve.Fori(0, NH // HB) as g:
                for j in range(HB):
                    head(g * HB + j, j)
            dve.wait_ge(s_x1, NH)

            def stage_lo(t, par):
                dve.wait_ge(s_xh, t + 1)
                for k in range(KL):
                    v.scalar_tensor_tensor(xstage[:, par, 1, k].rearrange("p b h -> p h b"),
                                           x1[:, k, :, bass.ds(t * TB, TB)], S_X,
                                           xstage[:, par, 0, k].rearrange("p b h -> p h b"),
                                           ALU.mult, ALU.subtract).then_inc(s_xl, 1)

            def lora_pairs(t):
                dve.wait_ge(s_ta, t + 1)
                for b in range(4):
                    rows = slice(32 * b, 32 * b + 32)
                    v.tensor_scalar(sel[rows].rearrange("p (q g) r -> p q (g r)", q=Q),
                                    ps[rows, 7, 0:Q * P].rearrange("p (q n) -> p q n", q=Q)
                                    [:, :, 2 * R * b:2 * R * b + 2 * R],
                                    S_T / G_SCALE, None, ALU.mult).then_inc(s_sel, 1)
                dve.wait_ge(s_sel, (t + 1) * 4)
                v.tensor_copy(val[:, :, 0, :], sel[:]).then_inc(s_val, 1)
                v.tensor_copy(val[:, :, 2, :], sel[:]).then_inc(s_val, 1)
                dve.wait_ge(s_val, t * 3 + 2)
                v.scalar_tensor_tensor(val[:, :, 1, :], sel[:], 1.0, val[:, :, 0, :], ALU.mult,
                                       ALU.subtract).then_inc(s_val, 1)
                dve.wait_ge(s_val, t * 3 + 3)
                wait(dve, s_tp, t)
                for j in range(2):
                    v.tensor_scalar(tt[:, :, j, :], val[:].rearrange("p n e r -> p n (e r)"),
                                    pair_sel[:, j:j + 1], None, ALU.mult).then_inc(s_tt, 1)

            def lora_down(t):
                dve.wait_ge(s_d, (t + 1) * FT)
                wait(dve, s_t2p, t)
                for b in range(4):
                    rows = slice(32 * b, 32 * b + 32)
                    v.tensor_scalar(t2[rows, :, 2 * R * b:2 * R * b + R], ps[rows, 4:6, R * b:R * b + R],
                                    S_T2 / O_SCALE, None, ALU.mult).then_inc(s_t2h, 1)
                dve.wait_ge(s_t2h, (t + 1) * 4)
                for b in range(4):
                    rows = slice(32 * b, 32 * b + 32)
                    v.scalar_tensor_tensor(t2[rows, :, 2 * R * b + R:2 * R * (b + 1)],
                                           ps[rows, 4:6, R * b:R * b + R], S_T2 / O_SCALE,
                                           t2[rows, :, 2 * R * b:2 * R * b + R],
                                           ALU.mult, ALU.subtract).then_inc(s_t2, 1)

            def down_turned(t):
                dve.wait_ge(s_t2p, t + 1)
                wait(dve, s_acc, t)
                v.tensor_copy(t2a[:], ps[:, 6, 0:P].bitcast(F16).rearrange("p (q n) -> p q n", q=Q))\
                    .then_inc(s_t2a, 1)

            def evacuate(t):
                dve.wait_ge(s_acc, t + 1)
                wait(dve, s_out, t * 16)
                v.tensor_scalar(out_sb[:, 1, :], ps[:, 3, :], 1 / O_SCALE, None, ALU.mult).then_inc(s_ev1, 1)

            def block_act(t, par, m):
                n = t * FT + m
                turn = (par + m) % 2
                rows = slice(0, min(P, FF - m * P))
                dve.wait_ge(s_sg, n + 1)
                v.scalar_tensor_tensor(af[rows, turn], ps[rows, turn, TOK:2 * TOK], S_ACT / G_SCALE,
                                       sg[rows, turn], ALU.mult, ALU.mult).then_inc(s_af, 1)
                dve.wait_ge(s_ah, n + 1)
                v.tensor_tensor(act_hl[rows, m, 1], af[rows, turn], act_hl[rows, m, 0],
                                ALU.subtract).then_inc(s_al, 1)

            def tile(t, par, first, last):
                for m in range(FT):
                    block_act(t, par, m)
                    if m == 0 and not first:
                        lora_down(t - 1)
                    if m == 1 and not first:
                        down_turned(t - 1)
                    if m == 2 and not first:
                        evacuate(t - 1)
                    if m == 3 and not last:
                        stage_lo(t + 1, 1 - par)
                    if m == 6 and not last:
                        lora_pairs(t + 1)

            stage_lo(0, 0)
            lora_pairs(0)
            tile(0, 0, True, False)
            with dve.Fori(0, (NT - 2) // 2) as g:
                tile(g * 2 + 1, 1, False, False)
                tile(g * 2 + 2, 0, False, False)
            tile(NT - 1, 1, False, True)
            lora_down(NT - 1)
            down_turned(NT - 1)
            evacuate(NT - 1)

        @block.scalar
        def _(act):
            s = nc.scalar
            def split_piece(i):
                v, hi, _ = piece(i)
                act.wait_ge(s_li[i % 2], 16 * (i // 2 + 1))
                if i >= 2:
                    act.wait_ge(store_sem(i - 2), 16 * STORES[i - 2])
                s.activation(hi, v, ACT.Copy, scale=S_W).then_inc(s_lh, 1)
                act.wait_ge(s_lh, 2 * i + 1)
                s.activation(v, v, ACT.Copy, scale=S_W).then_inc(s_lh, 1)

            top, low = slice(0, NST), slice(NST, 2 * NST)
            act.wait_ge(s_mag, 1)
            s.activation(mag_t, mag_t, ACT.Exp).then_inc(s_a, 1)
            split_piece(0)
            act.wait_ge(s_v, V_STEP["theta"])
            s.activation(sin_t[:, :, 0:CA + 1], theta[:, :, 0:CA + 1], ACT.Sin).then_inc(s_a, 1)
            s.activation(sin_t[low, :, FAC2], theta[low, :, FAC2], ACT.Sin).then_inc(s_a, 1)
            act.wait_ge(s_v, V_STEP["abs_theta"])
            s.activation(cos_t[:, :, 0:CA + 1], abs_t[:, :, 0:CA + 1], ACT.Sin, bias=half_pi[:, 0:1],
                         scale=-1.0).then_inc(s_a, 1)
            s.activation(sin_t[top, :, FAC2], abs_t[top, :, FAC2], ACT.Sin, bias=half_pi[top, 0:1],
                         scale=-1.0).then_inc(s_a, 1)
            for i in range(1, N_FIRST):
                split_piece(i)

            def head(g, j, first):
                h = g * HB + j
                act.wait_ge(s_s[j], 16 * (g + 1))
                if not first:
                    act.wait_ge(s_y, h - 1)
                s.activation(toep[:, j % 2, :], s_ring[:, j, ::-1], ACT.Copy).then_inc(s_r, 1)
                act.wait_ge(s_w[j], 16 * (g + 1))
                s.activation(w_hi[:, bass.ds(h * WCH, WCH)], wring[:, j, :], ACT.Copy, scale=S_W).then_inc(s_wh, 1)

            act.wait_ge(s_k, 1)
            act.wait_ge(s_kd, 32)
            for j in range(HB):
                head(0, j, j < 2)
            with act.Fori(1, NH // HB) as g:
                for j in range(HB):
                    head(g, j, False)

            def stage_hi(t, par):
                if par == 0 and isinstance(t, int):
                    act.wait_ge(s_x1, NH)
                    act.wait_ge(s_wl, NH)
                else:
                    wait(act, s_acc, t - 1)
                s.activation(xstage[:, par, 0].rearrange("p k b h -> p k h b"),
                             x1[:, :, :, bass.ds(t * TB, TB)], ACT.Copy, scale=S_X).then_inc(s_xh, 1)

            def pairs_turned(t, par):
                act.wait_ge(s_tp, t + 1)
                wait(act, s_gu, (t - 1) * FT)
                s.activation(t_mov[0:3 * 2 * R, par].rearrange("p g q n -> p (g q n)"),
                             ps[0:3 * 2 * R, 6, 0:2 * P].bitcast(F16), ACT.Copy).then_inc(s_tm, 1)

            def evacuate(t):
                act.wait_ge(s_acc, t + 1)
                wait(act, s_out, t * 16)
                s.activation(out_sb[:, 0, :], ps[:, 2, :], ACT.Copy, scale=1 / O_SCALE).then_inc(s_ev0, 1)

            def block_act(t, par, m):
                n = t * FT + m
                turn = (par + m) % 2
                rows = slice(0, min(P, FF - m * P))
                act.wait_ge(s_gu, n + 1)
                wait(act, s_af, n - 1)
                s.activation(sg[rows, turn], ps[rows, turn, 0:TOK], ACT.Silu, scale=1 / G_SCALE).then_inc(s_sg, 1)
                act.wait_ge(s_af, n + 1)
                wait(act, s_d, n + 1 - FT)
                s.activation(act_hl[rows, m, 0], af[rows, turn], ACT.Copy).then_inc(s_ah, 1)

            def tile(t, par, first, last):
                for m in range(FT):
                    block_act(t, par, m)
                    if m == 2 and not first:
                        evacuate(t - 1)
                    if m == 3 and not last:
                        stage_hi(t + 1, 1 - par)
                    if m == 8 and not last:
                        pairs_turned(t + 1, 1 - par)

            stage_hi(0, 0)
            pairs_turned(0, 0)
            tile(0, 0, True, False)
            with act.Fori(0, (NT - 2) // 2) as g:
                tile(g * 2 + 1, 1, False, False)
                tile(g * 2 + 2, 0, False, False)
            tile(NT - 1, 1, False, True)
            evacuate(NT - 1)

        @block.tensor
        def _(pe):
            mm = nc.tensor.matmul
            pe.wait_ge(s_v, V_STEP["drow"])
            for i in range(2):
                mm(ps[0:CA, 4 + i, :], onehot, drow[0:1].rearrange("p h c -> p (h c)")[:, 512 * i:512 * i + 512],
                   start=True, stop=False, skip_group_check=True)
            for h in range(NH):
                c0 = CC * (h % 16)
                last = mm(ps[0:CA, 4 + h // 16, c0:c0 + CC], g1[:, h, :], fac2[:, h, :],
                          start=False, stop=True, skip_group_check=True)
            last.then_inc(s_k, 1)

            def head(h, j, first):
                pe.wait_ge(s_r, h + 1)
                if not first:
                    pe.wait_ge(s_ym, h - 1)
                for lk in range(KL):
                    for mk in range(lk + 1):
                        last = mm(ps[:, j % 2, lk * P:(lk + 1) * P], toep[:, j % 2, (lk - mk) * P:(lk - mk + 1) * P],
                                  x1[:, mk, bass.ds(h, 1), :].rearrange("p a b -> p (a b)"),
                                  start=(mk == 0), stop=(mk == lk))
                last.then_inc(s_y, 1)

            pe.wait_ge(s_x, 16 * (NH // HB))
            for j in range(HB):
                head(j, j, j < 2)
            with pe.Fori(1, NH // HB) as g:
                for j in range(HB):
                    head(g * HB + j, j, False)

            def lora_a(t, par):
                pe.wait_ge(s_xl, (t + 1) * KL)
                pe.wait_ge(s_ga, 16 * TB * (t + 1))
                wait(pe, s_tt, t * 2)
                if isinstance(t, int) and t == 0:
                    pe.wait_ge(s_wl, NH)
                for q in range(Q):
                    for k in range(KL):
                        for xe, ae in ((0, 0), (0, 1), (1, 0)):
                            last = mm(ps[:, 7, q * P:(q + 1) * P],
                                      xstage[:, par, xe, k, 4 * q:4 * q + 4, :].rearrange("p b h -> p (b h)"),
                                      a_buf[:, 4 * q:4 * q + 4, ae, k, :],
                                      start=(k == 0 and xe == 0 and ae == 0), stop=(k == KL - 1 and xe == 1))
                last.then_inc(s_ta, 1)

            def turn_pairs(t):
                pe.wait_ge(s_tt, (t + 1) * 2)
                wait(pe, s_t2a, t - 1)
                for g in range(2):
                    for q in range(Q):
                        last = nc.tensor.transpose(ps[0:3 * 2 * R, 6, (g * Q + q) * 64:(g * Q + q) * 64 + 64].bitcast(F16),
                                                   tt[:, q * 2 + g].rearrange("p j n -> p (j n)"), ident[:])
                last.then_inc(s_tp, 1)

            def gate_up(t, par, m, between=None):
                n = t * FT + m
                turn = (par + m) % 2
                f = min(P, FF - m * P)
                wait(pe, s_af, n - 1)
                if m * P == 0:
                    pe.wait_ge(s_gb[0], 16 * TB * (t + 1))
                if m * P == FH0:
                    pe.wait_ge(s_gb[1], 16 * TB * (t + 1))
                half = 1 if m * P >= FH0 else 0
                fo = m * P - half * FH0
                for g in range(2):
                    o = ps[0:f, turn, g * TOK:(g + 1) * TOK]
                    for k in range(KL):
                        c0 = (g * KL + k) * FF + m * P
                        for we, xe in ((0, 0), (0, 1), (1, 0)):
                            w = (w_hi, w_lo)[we]
                            mm(o, w[:, c0:c0 + f], xstage[:, par, xe, k].rearrange("p b h -> p (b h)"),
                               start=(k == 0 and we == 0 and xe == 0), stop=False)
                    if m == 0 and g == 0:
                        if between is not None:
                            between()
                        pe.wait_ge(s_tm, t + 1)
                    for j in range(4):
                        last = mm(ps[0:f, turn, g * TOK + 64 * j:g * TOK + 64 * j + 64],
                                  b_half[half][0:3 * 2 * R, j, g, fo:fo + f],
                                  t_mov[0:3 * 2 * R, par, g, j // 2, 64 * (j % 2):64 * (j % 2) + 64],
                                  start=False, stop=(j == 3))
                last.then_inc(s_gu, 1)

            def down(t, m):
                kf = min(P, FF - m * P)
                pe.wait_ge(s_al, t * FT + m + 1)
                if m == 0:
                    pe.wait_ge(s_gad, 16 * TB * (t + 1))
                    wait(pe, s_ev0, t)
                    wait(pe, s_ev1, t)
                    wait(pe, s_t2, t * 4)
                for q in range(Q):
                    w = slice(WD0 + m * NL, WD0 + (m + 1) * NL)
                    for ae, we in ((0, 0), (0, 1), (1, 0)):
                        a = act_hl[0:kf, m, ae, q * P:(q + 1) * P]
                        first = m == 0 and ae == 0 and we == 0
                        mm(ps[:, 2 + q, :], a, (w_hi, w_lo)[we][0:kf, w], start=first, stop=False)
                        last = mm(ps[:, 4 + q, 0:4 * R], a, ad_buf[0:kf, 4 * q:4 * q + 4, we, m, :],
                                  start=first, stop=(m == FT - 1 and ae == 1))
                last.then_inc(s_d, 1)

            def turn_down(t):
                pe.wait_ge(s_t2, (t + 1) * 4)
                wait(pe, s_tm, t + 1)
                for q in range(Q):
                    last = nc.tensor.transpose(ps[:, 6, q * 64:q * 64 + 64].bitcast(F16), t2[:, q, :], ident[:])
                last.then_inc(s_t2p, 1)

            def finish(t, par):
                pe.wait_ge(s_t2a, t + 1)
                pe.wait_ge(s_gbd, 16 * TB * (t + 1))
                for q in range(Q):
                    for e in range(2):
                        mm(ps[:, 2 + q, :], t2a[:, q, :], bd_buf[:, q, e, :], start=False, stop=False)
                    for k in range(KL):
                        for e in range(2):
                            last = mm(ps[:, 2 + q, k * P:(k + 1) * P], xstage[:, par, e, k, 4 * q:4 * q + 4, :].rearrange("p b h -> p (b h)"),
                                      ident_x[:], start=False, stop=(k == KL - 1 and e == 1))
                last.then_inc(s_acc, 1)

            def tile(t, par, first, last):
                for m in range(FT):
                    gate_up(t, par, m, (lambda: turn_pairs(0)) if first and m == 0 else None)
                    if not first:
                        if m == 0:
                            down(t - 1, FT - 1)
                        if m == 1:
                            turn_down(t - 1)
                        if m == 2:
                            finish(t - 1, 1 - par)
                    if m == 6 and not last:
                        lora_a(t + 1, 1 - par)
                    if m == 8 and not last:
                        turn_pairs(t + 1)
                    for d in DOWN_AT.get(m, ()):
                        down(t, d)

            DOWN_AT = {4: (0, 1, 2), 5: (3, 4), 6: (5,), 7: (6,), 8: (7,), 9: (8,), 10: (9,)}
            lora_a(0, 0)
            tile(0, 0, True, False)
            with pe.Fori(0, (NT - 2) // 2) as g:
                tile(g * 2 + 1, 1, False, False)
                tile(g * 2 + 2, 0, False, False)
            tile(NT - 1, 1, False, True)
            down(NT - 1, FT - 1)
            turn_down(NT - 1)
            finish(NT - 1, 1)

        @block.sync
        def _(sp):
            sp.dma_start(params, par).then_inc(s_par, 16)
            sp.dma_start(dval, dvec.unsqueeze(0)).then_inc(s_par, 16)
            sp.dma_start(leni, length.partition_broadcast(P)).then_inc(s_par, 16)
            sp.dma_start(adapter_sb[:], adapter).then_inc(s_par, 16)
            for g in range(NH // HB):
                sp.dma_start(x1[:, :, g * HB:(g + 1) * HB, :],
                             xt[:, g].rearrange("p k (h b) -> p k h b", h=HB)).then_inc(s_x, 16)
            sp.wait_ge(s_pool, 1)
            sp.dma_start(krev[:, NL:KROW], zrow).then_inc(s_kd, 16)
            sp.wait_ge(s_v, V_KSB[0])
            sp.dma_start(krev[:, 0:NL].rearrange("h (a c) -> a h c", a=CA), ksb[0:CA]).then_inc(s_kd, 16)
            sp.wait_ge(s_kd, 32)

            def head_loads(h, slot, first):
                if not first:
                    sp.wait_ge(s_r, h - HB + 1)
                sp.dma_start(s_ring[:, slot, :], strip(h)).then_inc(s_s[slot], 16)
                if not first:
                    sp.wait_ge(s_wl, h - HB + 1)
                sp.dma_start(wring[:, slot, :], wall[:, bass.ds(h * WCH, WCH)]).then_inc(s_w[slot], 16)

            def strip(h):
                return bass.AP(krev.tensor, h * KROW, [[1, P], [1, NL]])

            for j in range(HB):
                head_loads(j, j, True)
            with sp.Fori(1, NH // HB) as g:
                for j in range(HB):
                    head_loads(g * HB + j, j, False)

            for i in range(N_FIRST - 2, N_FIRST):
                sp.wait_ge(store_sem(i), 16 * STORES[i])

            def indices(t):
                return [sp.value_load(adapter_sb[:, bass.ds(t * TB + j, 1)], min_val=0, max_val=NAD - 1)
                        for j in range(TB)]

            def fetch_a(t, idx):
                wait(sp, s_ta, t)
                for j, a in enumerate(idx):
                    sp.dma_start(a_buf[:, j].rearrange("p e k n -> p e (k n)"),
                                 a_scr[bass.ds(a, 1)].squeeze(0)).then_inc(s_ga, 16)

            def fetch_rest(t, idx, prev):
                for half in range(2):
                    if prev:
                        sp.wait_ge(s_gu, (t - 1) * FT + (FH0 // P if half == 0 else FT))
                    f0 = FH0 * half
                    for j, a in enumerate(idx):
                        r0 = 3 * R * (j % 2)
                        sp.dma_start(b_half[half][r0:r0 + 3 * R, j // 2],
                                     b_scr[bass.ds(a, 1), :, :, :, f0:f0 + FHS[half]]
                                     .rearrange("a e r g f -> (a e r) g f")).then_inc(s_gb[half], 16)
                if prev:
                    sp.wait_ge(s_d, t * FT)
                else:
                    for i in range(len(LPARTS) - 2, len(LPARTS)):
                        sp.wait_ge(store_sem(i), 16 * STORES[i])
                for j, a in enumerate(idx):
                    sp.dma_start(ad_buf[:, j].rearrange("p e k n -> p e (k n)"),
                                 ad_scr[bass.ds(a, 1)].squeeze(0)).then_inc(s_gad, 16)
                if prev:
                    sp.wait_ge(s_acc, t)
                for j, a in enumerate(idx):
                    r0 = 2 * R * (j % 4)
                    sp.dma_start(bd_buf[r0:r0 + 2 * R, j // 4],
                                 bd_scr[bass.ds(a, 1)].rearrange("a e r g f -> (a e r) g f")).then_inc(s_gbd, 16)

            def store(t):
                sp.wait_ge(s_ev0, t + 1)
                sp.wait_ge(s_ev1, t + 1)
                sp.dma_start(out[bass.ds(t * TOK, TOK), :].rearrange("(q p) n -> p q n", q=Q), out_sb[:])\
                    .then_inc(s_out, 16)

            first = indices(0)
            fetch_a(0, first)
            fetch_rest(0, first, False)
            second = indices(1)
            fetch_a(1, second)
            fetch_rest(1, second, True)
            with sp.Fori(2, NT) as t:
                idx = indices(t)
                store(t - 2)
                fetch_a(t, idx)
                fetch_rest(t, idx, True)
            store(NT - 2)
            store(NT - 1)
            sp.wait_ge(s_out, 16 * NT)

        @block.gpsimd
        def _(pool):
            g = nc.gpsimd
            g.memset(zrow, 0.0).then_inc(s_pool, 1)
            g.iota(lags[:, 0:CA], [[-CC, CA]], base=CC * (CA - 1), channel_multiplier=0,
                   allow_small_or_imprecise_dtypes=True).then_inc(s_pool, 1)
            g.iota(lags[:, FAC2], [[-1, CC]], base=CC - 1, channel_multiplier=0,
                   allow_small_or_imprecise_dtypes=True).then_inc(s_pool, 1)
            g.memset(lags[:, STEP:STEP + 1], 1.0).then_inc(s_pool, 1)
            g.iota(ioti.rearrange("p (k b) -> p k b", k=KL), [[P, KL], [0, NB]], base=0, channel_multiplier=1,
                   allow_small_or_imprecise_dtypes=True).then_inc(s_pool, 1)
            g.memset(onehot, 0.0).then_inc(s_pool, 1)
            g.memset(ident[:], 0.0).then_inc(s_pool, 1)
            g.memset(ident_x[:], 0.0).then_inc(s_pool, 1)
            g.memset(drow[0:1], 0.0).then_inc(s_pool, 1)
            g.memset(tt[:], 0.0).then_inc(s_pool, 1)
            g.memset(t2[:], 0.0).then_inc(s_pool, 1)
            pool.wait_ge(s_pool, 11)
            g.memset(onehot[:, CA - 1:CA], 1.0).then_inc(s_pool, 1)
            for m, v in ((ident, 1.0), (ident_x, O_SCALE / S_X)):
                g.affine_select(out=m[:], in_=m[:], compare_op=ALU.not_equal, fill=v, base=0,
                                pattern=[[-1, P]], channel_multiplier=1).then_inc(s_pool, 1)
            g.memset(half_pi[:], TWO_PI / 4).then_inc(s_pool, 1)

            pool.wait_ge(s_v, V_STEP["d_re"])
            g.tensor_tensor(mag_t, d_re.unsqueeze(2).to_broadcast([P, NH, NE]),
                            lags.unsqueeze(1).to_broadcast([P, NH, NE]), ALU.mult).then_inc(s_mag, 1)

            load_piece(pool, 0)
            load_piece(pool, 1)
            for i, (kind, part, n) in enumerate(LPARTS):
                v, hi, lo = piece(i)
                if i < N_FIRST:
                    pool.wait_ge(s_lh, 2 * (i + 1))
                else:
                    pool.wait_ge(s_li[i % 2], 16 * (i // 2 + 1))
                    g.tensor_scalar(v, v, S_W, None, ALU.mult).then_inc(s_lc, 1)
                    for_slot = STORES[i - 2] * 16
                    if i >= N_FIRST + 2:
                        pool.wait_ge(store_sem(i - 2), for_slot)
                    pool.wait_ge(s_lc, LC[i] - 2)
                    g.tensor_copy(hi, v).then_inc(s_lc, 1)
                    pool.wait_ge(s_lc, LC[i] - 1)
                g.tensor_tensor(lo, v, hi, ALU.subtract).then_inc(s_lc, 1)
                if i + 2 < len(LPARTS):
                    load_piece(pool, i + 2)
                pool.wait_ge(s_lc, LC[i])
                if kind == "A":
                    a0 = part * (NAD // 2)
                    for e, src in enumerate((hi, lo)):
                        pool.dma_start(a_scr[a0:a0 + NAD // 2, :, e, :].rearrange("a p n -> p a n"),
                                       src.rearrange("p (a n) -> p a n", a=NAD // 2)).then_inc(store_sem(i), 16)
                elif kind == "B":
                    blk, gu = part
                    for e, src in enumerate((hi, hi, lo)):
                        for_a = b_scr[8 * blk:8 * blk + 8, e, :, gu, :]
                        pool.dma_start(for_a, src).then_inc(store_sem(i), 16)
                elif kind == "Ad":
                    for e, src in enumerate((hi, lo)):
                        pool.dma_start(ad_scr[4 * part:4 * part + 4, :, e, :].rearrange("a p n -> p a n"),
                                       src.rearrange("p (a n) -> p a n", a=4)).then_inc(store_sem(i), 16)
                else:
                    for d in range(2):
                        for e, src in enumerate((hi, lo)):
                            pool.dma_start(bd_scr[8 * part:8 * part + 8, d, :, e, :], src).then_inc(store_sem(i), 16)


def kernel(x, itok_B_78_3631, itok_B_2_6, L0_cond_log_dt, L0_cond_C, L0_cond_log_A_real, L0_cond_A_imag, L0_cond_D,
           L1_cond_W_gate, L1_cond_W_up, L1_cond_W_down, L1_cond_A_gate, L1_cond_B_gate, L1_cond_A_up,
           L1_cond_B_up, L1_cond_A_down, L1_cond_B_down):
    import numpy as np
    import concourse.bacc as bacc
    from concourse.bass_utils import run_bass_kernel_spmd

    def arr(a):
        return np.asarray(a)

    xt = arr(x).transpose(2, 1, 0).reshape(KL, P, NH // 4, 4 * NB).transpose(1, 2, 0, 3)
    wall = np.zeros((P, NW), np.float32)
    for g, w in enumerate((L1_cond_W_gate, L1_cond_W_up)):
        wall[:, g * KL * FF:(g + 1) * KL * FF] = arr(w).T.reshape(KL, P, FF).transpose(1, 0, 2).reshape(P, KL * FF)
    wd = np.zeros((FT * P, NL), np.float32)
    wd[:FF] = arr(L1_cond_W_down).T
    wall[:, WD0:] = wd.reshape(FT, P, NL).transpose(1, 0, 2).reshape(P, FT * NL)
    a_gu = np.stack([arr(L1_cond_A_gate)[0], arr(L1_cond_A_up)[0]])
    a_gu = a_gu.reshape(2, NAD, R, KL, P).transpose(4, 1, 3, 0, 2).reshape(P, 2, NLA)
    parts = [a_gu[:, 0], a_gu[:, 1]]
    b_t = [arr(b)[0].transpose(0, 2, 1).reshape(NAD * R, FF) for b in (L1_cond_B_gate, L1_cond_B_up)]
    parts += [b_t[gu][blk * P:(blk + 1) * P] for blk in range(2) for gu in range(2)]
    ad = np.zeros((NAD, R, FT * P), np.float32)
    ad[:, :, :FF] = arr(L1_cond_A_down)[0]
    ad = ad.reshape(NAD, R, FT, P).transpose(3, 0, 2, 1).reshape(P, 4, 4 * FT * R)
    parts += [ad[:, g] for g in range(4)]
    bd = arr(L1_cond_B_down)[0].transpose(0, 2, 1).reshape(NAD * R, NL)
    parts += [bd[:P], bd[P:]]
    c = arr(L0_cond_C)
    par = [np.broadcast_to(arr(L0_cond_log_dt), (NST, NH)), arr(L0_cond_log_A_real).T, arr(L0_cond_A_imag).T,
           c[:, :, 0].T, c[:, :, 1].T]
    par = np.tile(np.concatenate(par, axis=1), (2, 1))
    ins = {
        "xt": xt, "wall": wall, "lora": np.concatenate(parts, axis=1),
        "par": par, "dvec": arr(L0_cond_D),
        "length": arr(itok_B_78_3631), "adapter": arr(itok_B_2_6).reshape(1, NB),
    }
    nc = bacc.Bacc("TRN2", target_bir_lowering=False, num_devices=1)
    arrays, aps = {}, {}
    for name, a in ins.items():
        a = np.ascontiguousarray(a)
        arrays[name] = a
        aps[name] = nc.dram_tensor(name, a.shape, mybir.dt.from_np(a.dtype), kind="ExternalInput").ap()
    y = nc.dram_tensor("y", (NB * NH, NL), F32, kind="ExternalOutput").ap()
    build(nc, out=y, **aps)
    r = run_bass_kernel_spmd(nc, [arrays], core_ids=[0])
    return r.results[0]["y"].reshape(NB, NH, NL)
```

```python
from contextlib import ExitStack

import concourse.bass as bass
from concourse import mybir

F32 = mybir.dt.float32
F16 = mybir.dt.float16
I32 = mybir.dt.int32
ALU = mybir.AluOpType
ACT = mybir.ActivationFunctionType

P = 128
NB, NH, NL = 128, 32, 512
NST = 64
FF = 1376
R = 16
NAD = 16
KL = NL // P
FT = (FF + P - 1) // P
FH0 = 6 * P
FH1 = FF - FH0
FHS = [FH0, FH1]
CA, CC = 16, 32
KROW = NL + P
NW = 2 * KL * FF + FT * NL
WD0 = 2 * KL * FF
WM = 2 * KL * P
EARLY = 8
WCH = EARLY * WM // NH
LATE = [(c, min(NL, WD0 - c)) for c in range(EARLY * WM, WD0, NL)]
N_GU = len(LATE)
LATE += [(WD0 + m * NL, NL) for m in range(FT)]
TB = 8
NT = NB // TB
TOK = TB * NH
Q = TOK // P
assert EARLY * WM % NH == 0 and WCH <= NL

S_X, S_W, S_T, S_ACT, S_T2 = 8.0, 256.0, 4.0, 4.0, 2.0
G_SCALE = S_X * S_W
O_SCALE = S_ACT * S_W
assert S_T * S_W == 0.5 * G_SCALE and S_T2 * S_W == 0.5 * O_SCALE

TWO_PI = 6.283185307179586
PI_HI = 6.28125
PI_LO = TWO_PI - PI_HI
INV_HI = 0.15915493667125702
INV_LO = 1 / TWO_PI - INV_HI
TURN = 6.283185
LN2 = 0.6931471805599453
LN2_HI = 0.693145751953125
LN2_LO = LN2 - LN2_HI
MAGIC = 12582912.0
EXP_C = [1 / 5040, 1 / 720, 1 / 120, 1 / 24, 1 / 6, 0.5, 1.0, 1.0]

NLA = 2 * KL * R * NAD // 4
NLB = FF // 2
OFF_B = 4 * NLA
OFF_AD = OFF_B + 8 * NLB
NLD = 4 * FT * R
OFF_BD = OFF_AD + 4 * NLD


def build(nc, xt, wall, lora, par, dvec, length, adapter, out):
    ctx = ExitStack()
    with ctx:
        def sb(name, shape, dt):
            return ctx.enter_context(nc.sbuf_tensor(name, shape, dt))

        def sem(name):
            return ctx.enter_context(nc.semaphore(name))

        krev = nc.dram_tensor("krev", [NH, KROW], F32, kind="Internal").ap()
        a_scr = nc.dram_tensor("a_scr", [NAD, P, 2, 2 * KL * R], F16, kind="Internal").ap()
        b_scr = nc.dram_tensor("b_scr", [NAD, 3, R, 2, FF], F16, kind="Internal").ap()
        ad_scr = nc.dram_tensor("ad_scr", [NAD, P, 2, FT * R], F16, kind="Internal").ap()
        bd_scr = nc.dram_tensor("bd_scr", [NAD, 2, R, 2, NL], F16, kind="Internal").ap()

        w_hi = sb("w_hi", [P, NW], F16)
        w_lo = sb("w_lo", [P, NW], F16)
        x1 = sb("x1", [P, KL, NH, NB], F32)
        up_lora = sb("up_lora", [P, 4 * 2 * FF], F16)
        b_half = [up_lora[:, 0:8 * FH0].rearrange("p (j g f) -> p j g f", j=4, g=2),
                  up_lora[:, 8 * FH0:8 * FF].rearrange("p (j g f) -> p j g f", j=4, g=2)]
        a_buf = sb("a_buf", [P, TB, 2, KL, 2 * R], F16)
        ad_buf = sb("ad_buf", [P, TB, 2, FT, R], F16)
        down_lora = sb("down_lora", [P, 2 * FT * R * TB], F16)
        bd_buf = down_lora[:, 0:Q * 2 * NL].rearrange("p (q e n) -> p q e n", q=Q, e=2)
        xstage = sb("xstage", [P, 2, 2, KL, TB, NH], F16)
        wring = sb("wring", [P, 4, NL], F32)
        act_hl = sb("act_hl", [P, FT, 2, TOK], F16)
        s_ring = act_hl[:, :, :, :].rearrange("p m e t -> p (m e t)")[:, 0:4 * 2 * NL].bitcast(F32)\
            .rearrange("p (s n) -> p s n", s=4)
        toep = xstage[:, 1].rearrange("p e k b h -> p (e k b h)").bitcast(F32).rearrange("p (s n) -> p s n", s=2)
        t_mov = sb("t_mov", [P, 2, 2, Q, P], F16)
        sg = sb("sg", [P, 2, TOK], F32)
        af = sb("af", [P, 2, TOK], F32)
        out_sb = sb("out_sb", [P, Q, NL], F32)
        mask = sg[:].rearrange("p a n -> p (a n)").rearrange("p (k b) -> p k b", k=KL)
        ym = out_sb
        sel = sb("sel", [P, Q * 2, R], F32)
        val = sb("val", [P, Q * 2, 3, R], F16)
        tt = sb("tt", [P, Q * 2, 2, 3 * R], F16)
        t2 = sb("t2", [P, Q, P], F16)
        t2a = sb("t2a", [P, Q, P], F16)
        ident = sb("ident", [P, P], F16)
        ident_x = sb("ident_x", [P, P], F16)
        pair_sel = sb("pair_sel", [P, 2], F32)
        half_pi = sb("half_pi", [P, 1], F32)
        adapter_sb = sb("adapter_sb", [1, NB], I32)

        wf = [w_hi[:, :].bitcast(F32), w_lo[:, :].bitcast(F32)]
        NE = CA + CC + 1
        NX = NH * NE

        def tmp(i, n0, shape):
            n = 1
            for s in shape:
                n *= s
            v = wf[i][:, n0:n0 + n]
            if len(shape) == 2:
                v = v.rearrange("p (a b) -> p a b", a=shape[0])
            return v

        theta = tmp(0, 0, [NH, NE])
        turns = tmp(0, NX, [NH, NE])
        sin_t = tmp(0, 2 * NX, [NH, NE])
        cos_t = tmp(0, 3 * NX, [NH, NE])
        mag_t = tmp(0, 4 * NX, [NH, NE])
        FAC1, STEP, FAC2 = slice(0, CA), CA, slice(CA + 1, NE)
        abs_t = tmp(1, 0, [NH, NE])
        fac2 = tmp(1, NX, [NH, CC])
        g1 = tmp(1, 2 * NX, [NH, CA])
        g2 = tmp(1, 2 * NX + NH * CA, [NH, CA])
        ksb = tmp(1, 2 * NX + 2 * NH * CA + NH * CC, [NH, CC])
        at1 = 2 * NX + 2 * NH * CA + 2 * NH * CC
        lags = wf[1][:, at1:at1 + NE]
        ioti = wf[1][:, at1 + 64:at1 + 64 + KL * NB]
        leni = wf[1][:, at1 + 64 + KL * NB:at1 + 64 + KL * NB + NB].bitcast(I32)
        lenf = wf[1][:, at1 + 64 + KL * NB + NB:at1 + 64 + KL * NB + 2 * NB]
        at1 += 64 + KL * NB + 2 * NB
        zrow = wf[1][0:NH, at1:at1 + P]
        onehot = wf[1][0:1, at1 + P:at1 + P + CA]
        dval = wf[1][0:1, at1 + P + CA:at1 + P + CA + NH]
        small0 = at1 + P + CA + NH
        s0 = [0]

        def col(n=NH):
            s0[0] += n
            assert small0 + s0[0] <= NW // 2
            return wf[1][:, small0 + s0[0] - n:small0 + s0[0]]
        params = col(5 * NH)
        ex_in = params[:, 0:2 * NH]
        a_im, c_re, c_im = [params[:, i * NH:(i + 1) * NH] for i in (2, 3, 4)]
        ex_k, ex_r, ex_p, ex_o = [col(2 * NH) for _ in range(4)]
        eg_k, eg_r, eg_p, eg_u, eg_o, t_im = [col() for _ in range(6)]
        d_re, d_im, den, u1, u2 = [col() for _ in range(5)]
        e2, w2, pq = [col(2 * NH) for _ in range(3)]
        a4, c4, m4 = [tmp(0, 5 * NX + i * 4 * NH, [4 * NH]) for i in range(3)]
        assert 5 * NX + 3 * 4 * NH <= NW // 2
        a_re = a4[:, 0:NH]
        e_re, e_im = e2[:, 0:NH], e2[:, NH:2 * NH]
        coef_p, coef_q = pq[:, 0:NH], pq[:, NH:2 * NH]

        def term(x4, out, i):
            return x4[:, (2 * out + i) * NH:(2 * out + i + 1) * NH]

        ps = ctx.enter_context(nc.psum_tensor("ps", [P, 8, 512], F32))

        s_par = sem("s_par")
        s_x = sem("s_x")
        s_x2 = sem("s_x2")
        s_pool = sem("s_pool")
        s_v = sem("s_v")
        s_a = sem("s_a")
        s_k = sem("s_k")
        s_kd = sem("s_kd")
        assert FT % 2 == 1
        HB = 4
        HT = 8
        X_EARLY = NH // HB - 1
        SPLIT, SPLIT_FIRST = ((1, 3), 5), ((4, 6), 7)
        SPLIT_AT = {1: (0,), 2: (1, 2), 3: (3,), 4: (4, 5), 5: (6, 7), 6: (8,), 7: (9, 10), 8: (11, 12), 9: (13, 14),
                    10: (15, 16)}
        assert sorted(i for c in SPLIT_AT.values() for i in c) == list(range(len(LATE)))
        BD_AT = (2, 6)
        assert NH // HT * 2 == 8
        s_s = [sem(f"s_s{i}") for i in range(HB)]
        s_r = sem("s_r")
        s_w = [sem(f"s_w{i}") for i in range(HB)]
        s_y = sem("s_y")
        s_ym = sem("s_ym")
        s_x1 = sem("s_x1")
        s_wh = sem("s_wh")
        s_wl = sem("s_wl")
        s_ai = [sem(f"s_ai{i}") for i in range(4)]
        s_ah0 = sem("s_ah0")
        s_al0 = sem("s_al0")
        s_as = sem("s_as")
        s_bi = [sem(f"s_bi{i}") for i in range(2)]
        s_bh = sem("s_bh")
        s_bl = sem("s_bl")
        s_bs = [sem(f"s_bs{i}") for i in range(2)]
        s_adi = sem("s_adi")
        s_adh = sem("s_adh")
        s_adl = sem("s_adl")
        s_ads = sem("s_ads")
        s_bdi = sem("s_bdi")
        s_bdh = sem("s_bdh")
        s_bdl = sem("s_bdl")
        s_bds = sem("s_bds")
        s_g = sem("s_g")
        s_ga = sem("s_ga")
        s_gb = [sem(f"s_gb{i}") for i in range(2)]
        s_gad = sem("s_gad")
        s_gbd = sem("s_gbd")
        s_xh = sem("s_xh")
        s_xl = sem("s_xl")
        s_ta = sem("s_ta")
        s_tt = sem("s_tt")
        s_tp = sem("s_tp")
        s_tm = sem("s_tm")
        s_sel = sem("s_sel")
        s_val = sem("s_val")
        s_gu = sem("s_gu")
        s_sg = sem("s_sg")
        s_af = sem("s_af")
        s_ah = sem("s_ah")
        s_al = sem("s_al")
        s_d = sem("s_d")
        s_t2h = sem("s_t2h")
        s_t2 = sem("s_t2")
        s_t2p = sem("s_t2p")
        s_t2a = sem("s_t2a")
        s_acc = sem("s_acc")
        s_ev0 = sem("s_ev0")
        s_ev1 = sem("s_ev1")
        s_out = sem("s_out")

        def wait(eng, s, v):
            if not isinstance(v, int) or v > 0:
                eng.wait_ge(s, v)

        block = ctx.enter_context(nc.Block())
        NPAR = 4

        def parts(flat, n):
            return flat[:, 0:2 * n].bitcast(F32), flat[:, 2 * n:3 * n], flat[:, 3 * n:4 * n]

        def piece_a(i):
            return parts(up_lora[:, 2 * FF * i:2 * FF * (i + 1)], NLA)

        def piece_b(blk):
            return parts(up_lora[:, 2 * FF * blk:2 * FF * (blk + 1)], NLB)

        def piece_ad():
            return parts(ad_buf[:].rearrange("p b e k r -> p (b e k r)"), NLD)

        def piece_bd():
            return parts(down_lora[:, :], NL)

        V_STEP = {}
        V_KSB = [0]
        G_STEP = {"exp": 32, "mag": 33}

        def vector_part_a(dve, v):
            n = [0]

            def step(ins, name=None):
                n[0] += 1
                ins.then_inc(s_v, 1)
                dve.wait_ge(s_v, n[0])
                if name:
                    V_STEP[name] = n[0]

            def exp_poly(x, k, r, p, o):
                step(v.tensor_scalar(k, x, 1 / LN2, -125.0, ALU.mult, ALU.max))
                step(v.tensor_scalar(k, k, 126.0, MAGIC, ALU.min, ALU.add))
                step(v.tensor_scalar(k, k, MAGIC, None, ALU.subtract))
                step(v.scalar_tensor_tensor(r, k, -LN2_HI, x, ALU.mult, ALU.add))
                step(v.scalar_tensor_tensor(r, k, -LN2_LO, r, ALU.mult, ALU.add))
                step(v.tensor_scalar(p, r, EXP_C[0], None, ALU.mult))
                for c in EXP_C[1:-1]:
                    step(v.scalar_tensor_tensor(p, p, c, r, ALU.add, ALU.mult))
                step(v.tensor_scalar(o.bitcast(I32), k, 127.0, 8388608.0, ALU.add, ALU.mult))
                step(v.scalar_tensor_tensor(o, p, 1.0, o, ALU.add, ALU.mult))

            def bc(x, m):
                return x.unsqueeze(2).to_broadcast([x.shape[0], NH, m])

            dve.wait_ge(s_par, 16 * NPAR)
            exp_poly(ex_in, ex_k, ex_r, ex_p, ex_o)
            dt = ex_o[:, 0:NH]
            step(v.tensor_scalar(a_re, ex_o[:, NH:2 * NH], -1.0, None, ALU.mult))
            step(v.tensor_scalar(term(a4, 1, 1), ex_o[:, NH:2 * NH], -1.0, None, ALU.mult))
            step(v.tensor_tensor(d_re, a_re, dt, ALU.mult), "d_re")
            step(v.tensor_tensor(d_im, a_im, dt, ALU.mult))
            step(v.tensor_scalar(u1, d_im, 1 / TWO_PI, MAGIC, ALU.mult, ALU.add))
            step(v.tensor_scalar(u1, u1, MAGIC, None, ALU.subtract))
            step(v.scalar_tensor_tensor(u2, u1, -PI_HI, d_im, ALU.mult, ALU.add))
            step(v.scalar_tensor_tensor(u2, u1, -PI_LO, u2, ALU.mult, ALU.add))
            step(v.tensor_scalar(t_im, u2, INV_HI, None, ALU.mult))
            step(v.scalar_tensor_tensor(t_im, u2, INV_LO, t_im, ALU.mult, ALU.add))
            dve.wait_ge(s_pool, 13)
            lagb = lags.unsqueeze(1).to_broadcast([P, NH, NE])
            step(v.tensor_tensor(theta, bc(t_im, NE), lagb, ALU.mult))
            step(v.tensor_scalar(turns, theta, MAGIC, None, ALU.add))
            step(v.scalar_tensor_tensor(theta, turns, MAGIC, theta, ALU.subtract, ALU.subtract), "theta")
            top, low = slice(0, NST), slice(NST, 2 * NST)
            step(v.scalar_tensor_tensor(abs_t[:, :, 0:CA + 1], theta[:, :, 0:CA + 1], -1.0, theta[:, :, 0:CA + 1],
                                        ALU.mult, ALU.max), "abs_1")
            step(v.scalar_tensor_tensor(abs_t[top, :, FAC2], theta[top, :, FAC2], -1.0, theta[top, :, FAC2],
                                        ALU.mult, ALU.max), "abs_2")
            step(v.tensor_tensor(u1, a_re, a_re, ALU.mult))
            step(v.tensor_tensor(u2, a_im, a_im, ALU.mult))
            step(v.tensor_tensor(u1, u1, u2, ALU.add))
            step(v.reciprocal(den, u1))
            dve.wait_ge(s_a, 2)
            dve.wait_ge(s_g, G_STEP["exp"])
            step(v.tensor_tensor(e_re, eg_o, cos_t[:, :, STEP], ALU.mult))
            step(v.tensor_tensor(e_im, eg_o, sin_t[:, :, STEP], ALU.mult))
            step(v.tensor_scalar(e_re, e_re, 1.0, None, ALU.subtract))

            def two_sums(out, x4, x2):
                step(v.tensor_tensor(m4.rearrange("p (o n) -> p o n", o=2), x4.rearrange("p (o n) -> p o n", o=2),
                                     x2.unsqueeze(1).to_broadcast([P, 2, 2 * NH]), ALU.mult))
                m = m4.rearrange("p (o i n) -> p o i n", o=2, i=2)
                step(v.tensor_tensor(out.rearrange("p (o n) -> p o n", o=2), m[:, :, 0], m[:, :, 1], ALU.add))

            two_sums(w2, a4, e2)
            w2v = w2.rearrange("p (o n) -> p o n", o=2)
            step(v.tensor_tensor(w2v, w2v, den.unsqueeze(1).to_broadcast([P, 2, NH]), ALU.mult))
            two_sums(pq, c4, w2)
            step(v.tensor_tensor(g1, bc(coef_p, CA), cos_t[:, :, FAC1], ALU.mult))
            step(v.tensor_tensor(g2, bc(coef_q, CA), sin_t[:, :, FAC1], ALU.mult))
            step(v.tensor_tensor(g1, g1, g2, ALU.add))
            dve.wait_ge(s_a, 5)
            step(v.tensor_tensor(g1, g1, mag_t[:, :, FAC1], ALU.mult))
            step(v.tensor_tensor(fac2, mag_t[:, :, FAC2], sin_t[:, :, FAC2], ALU.mult), "factors")
            step(v.tensor_copy(lenf, leni))
            step(v.tensor_tensor(mask, lenf.unsqueeze(1).to_broadcast([P, KL, NB]),
                                 ioti.rearrange("p (k b) -> p k b", k=KL), ALU.is_gt))
            step(v.memset(pair_sel[:], 0.0))
            for b in range(4):
                step(v.memset(pair_sel[32 * b:32 * b + 32, b % 2:b % 2 + 1], 1.0))
            dve.wait_ge(s_k, 1)
            step(v.tensor_copy(ksb[0:CA, 0:16].rearrange("p h c -> p (h c)"), ps[0:CA, 4, :]))
            V_KSB[0] = n[0]

        @block.vector
        def _(dve):
            v = nc.vector
            vector_part_a(dve, v)

            def head(h, j):
                dve.wait_ge(s_wh, h + 1)
                v.scalar_tensor_tensor(w_lo[:, bass.ds(h * WCH, WCH)], wring[:, j % HB, 0:WCH], S_W,
                                       w_hi[:, bass.ds(h * WCH, WCH)], ALU.mult, ALU.subtract).then_inc(s_wl, 1)
                dve.wait_ge(s_y, h + 1)
                v.tensor_tensor(ym[:, j % 2, :], ps[:, j % 2, :], mask.rearrange("p k b -> p (k b)"),
                                ALU.mult).then_inc(s_ym, 1)
                xs = x1[:, :, bass.ds(h, 1), :].rearrange("p k a b -> p k (a b)")
                dve.wait_ge(s_ym, h + 1)
                v.tensor_tensor(xs, xs, ym[:, j % 2, :].rearrange("p (k b) -> p k b", k=KL),
                                ALU.add).then_inc(s_x1, 1)

            def piece_b_lo(g, blk):
                raw, hi, lo = piece_b(blk)
                dve.wait_ge(s_bh, g * 2 + blk + 1)
                v.scalar_tensor_tensor(lo, raw, S_W, hi, ALU.mult, ALU.subtract).then_inc(s_bl, 1)

            def piece_ad_lo(g):
                raw, hi, lo = piece_ad()
                dve.wait_ge(s_adh, g + 1)
                v.scalar_tensor_tensor(lo, raw, S_W, hi, ALU.mult, ALU.subtract).then_inc(s_adl, 1)

            def heads(g, first):
                b_at, ad_at = SPLIT_FIRST if first else SPLIT
                for j in range(HT):
                    head(g * HT + j, j)
                    if j in b_at:
                        piece_b_lo(g, b_at.index(j))
                    if j == ad_at:
                        piece_ad_lo(g)

            dve.wait_ge(s_x, 16 * X_EARLY)
            heads(0, True)
            with dve.Fori(1, NH // HT - 1) as g:
                heads(g, False)
            dve.wait_ge(s_x2, 16)
            heads(NH // HT - 1, False)
            dve.wait_ge(s_x1, NH)

            def stage_lo(t, par):
                dve.wait_ge(s_xh, t + 1)
                for k in range(KL):
                    v.scalar_tensor_tensor(xstage[:, par, 1, k].rearrange("p b h -> p h b"),
                                           x1[:, k, :, bass.ds(t * TB, TB)], S_X,
                                           xstage[:, par, 0, k].rearrange("p b h -> p h b"),
                                           ALU.mult, ALU.subtract).then_inc(s_xl, 1)

            def lora_pairs(t):
                dve.wait_ge(s_ta, t + 1)
                for b in range(4):
                    rows = slice(32 * b, 32 * b + 32)
                    v.tensor_scalar(sel[rows].rearrange("p (q g) r -> p q (g r)", q=Q),
                                    ps[rows, 7, 0:Q * P].rearrange("p (q n) -> p q n", q=Q)
                                    [:, :, 2 * R * b:2 * R * b + 2 * R],
                                    S_T / G_SCALE, None, ALU.mult).then_inc(s_sel, 1)
                dve.wait_ge(s_sel, (t + 1) * 4)
                v.tensor_copy(val[:, :, 0, :], sel[:]).then_inc(s_val, 1)
                v.tensor_copy(val[:, :, 2, :], sel[:]).then_inc(s_val, 1)
                dve.wait_ge(s_val, t * 3 + 2)
                v.scalar_tensor_tensor(val[:, :, 1, :], sel[:], 1.0, val[:, :, 0, :], ALU.mult,
                                       ALU.subtract).then_inc(s_val, 1)
                dve.wait_ge(s_val, t * 3 + 3)
                wait(dve, s_tp, t)
                for j in range(2):
                    v.tensor_scalar(tt[:, :, j, :], val[:].rearrange("p n e r -> p n (e r)"),
                                    pair_sel[:, j:j + 1], None, ALU.mult).then_inc(s_tt, 1)

            def lora_down(t):
                dve.wait_ge(s_d, (t + 1) * FT)
                wait(dve, s_t2p, t)
                for b in range(4):
                    rows = slice(32 * b, 32 * b + 32)
                    v.tensor_scalar(t2[rows, :, 2 * R * b:2 * R * b + R], ps[rows, 4:6, R * b:R * b + R],
                                    S_T2 / O_SCALE, None, ALU.mult).then_inc(s_t2h, 1)
                dve.wait_ge(s_t2h, (t + 1) * 4)
                for b in range(4):
                    rows = slice(32 * b, 32 * b + 32)
                    v.scalar_tensor_tensor(t2[rows, :, 2 * R * b + R:2 * R * (b + 1)],
                                           ps[rows, 4:6, R * b:R * b + R], S_T2 / O_SCALE,
                                           t2[rows, :, 2 * R * b:2 * R * b + R],
                                           ALU.mult, ALU.subtract).then_inc(s_t2, 1)

            def down_turned(t):
                dve.wait_ge(s_t2p, t + 1)
                wait(dve, s_acc, t)
                v.tensor_copy(t2a[:], ps[:, 6, 0:P].bitcast(F16).rearrange("p (q n) -> p q n", q=Q))\
                    .then_inc(s_t2a, 1)

            def evacuate(t):
                dve.wait_ge(s_acc, t + 1)
                wait(dve, s_out, t * 16)
                v.tensor_scalar(out_sb[:, 1, :], ps[:, 3, :], 1 / O_SCALE, None, ALU.mult).then_inc(s_ev1, 1)

            def block_act(t, par, m):
                n = t * FT + m
                turn = (par + m) % 2
                rows = slice(0, min(P, FF - m * P))
                dve.wait_ge(s_sg, n + 1)
                v.scalar_tensor_tensor(af[rows, turn], ps[rows, turn, TOK:2 * TOK], S_ACT / G_SCALE,
                                       sg[rows, turn], ALU.mult, ALU.mult).then_inc(s_af, 1)
                dve.wait_ge(s_ah, n + 1)
                v.tensor_tensor(act_hl[rows, m, 1], af[rows, turn], act_hl[rows, m, 0],
                                ALU.subtract).then_inc(s_al, 1)

            def piece_bd_lo(i):
                raw, hi, lo = piece_bd()
                dve.wait_ge(s_bdh, i + 1)
                v.scalar_tensor_tensor(lo, raw, S_W, hi, ALU.mult, ALU.subtract).then_inc(s_bdl, 1)

            def late_lo(i):
                c0, n = LATE[i]
                dve.wait_ge(s_wh, NH + i + 1)
                v.scalar_tensor_tensor(w_lo[:, c0:c0 + n], wring[:, i % HB, 0:n], S_W, w_hi[:, c0:c0 + n], ALU.mult,
                                       ALU.subtract).then_inc(s_wl, 1)

            def tile(t, par, first, last):
                for m in range(FT):
                    block_act(t, par, m)
                    if first and m in BD_AT:
                        piece_bd_lo(BD_AT.index(m))
                    for d in SPLIT_AT.get(m, ()) if first else ():
                        late_lo(d)
                    if m == 0 and not first:
                        lora_down(t - 1)
                    if m == 1 and not first:
                        down_turned(t - 1)
                    if m == 2 and not first:
                        evacuate(t - 1)
                    if m == 3 and not last:
                        stage_lo(t + 1, 1 - par)
                    if m == 6 and not last:
                        lora_pairs(t + 1)

            stage_lo(0, 0)
            lora_pairs(0)
            tile(0, 0, True, False)
            with dve.Fori(0, (NT - 2) // 2) as g:
                tile(g * 2 + 1, 1, False, False)
                tile(g * 2 + 2, 0, False, False)
            tile(NT - 1, 1, False, True)
            lora_down(NT - 1)
            down_turned(NT - 1)
            evacuate(NT - 1)

        @block.scalar
        def _(act):
            s = nc.scalar

            def piece_a_hi(i):
                raw, hi, _ = piece_a(i)
                act.wait_ge(s_ai[i], 16)
                s.activation(hi, raw, ACT.Copy, scale=S_W).then_inc(s_ah0, 1)
                act.wait_ge(s_ah0, 2 * i + 1)
                s.activation(raw, raw, ACT.Copy, scale=S_W).then_inc(s_ah0, 1)

            def piece_b_hi(g, blk, first):
                raw, hi, _ = piece_b(blk)
                act.wait_ge(s_bi[blk], 16 * (g + 1))
                if not first:
                    act.wait_ge(s_bs[blk], 16 * 3 * g)
                s.activation(hi, raw, ACT.Copy, scale=S_W).then_inc(s_bh, 1)

            def piece_ad_hi(g, first):
                raw, hi, _ = piece_ad()
                act.wait_ge(s_adi, 16 * (g + 1))
                if not first:
                    act.wait_ge(s_ads, 16 * 2 * g)
                s.activation(hi, raw, ACT.Copy, scale=S_W).then_inc(s_adh, 1)

            top, low = slice(0, NST), slice(NST, 2 * NST)
            act.wait_ge(s_pool, 14)
            act.wait_ge(s_v, V_STEP["theta"])
            s.activation(sin_t[:, :, 0:CA + 1], theta[:, :, 0:CA + 1], ACT.Sin, scale=-TURN).then_inc(s_a, 1)
            act.wait_ge(s_v, V_STEP["abs_1"])
            s.activation(cos_t[:, :, 0:CA + 1], abs_t[:, :, 0:CA + 1], ACT.Sin, bias=half_pi[:, 0:1],
                         scale=-TURN).then_inc(s_a, 1)
            s.activation(sin_t[low, :, FAC2], theta[low, :, FAC2], ACT.Sin, scale=-TURN).then_inc(s_a, 1)
            act.wait_ge(s_v, V_STEP["abs_2"])
            s.activation(sin_t[top, :, FAC2], abs_t[top, :, FAC2], ACT.Sin, bias=half_pi[top, 0:1],
                         scale=-TURN).then_inc(s_a, 1)
            act.wait_ge(s_g, G_STEP["mag"])
            s.activation(mag_t, mag_t, ACT.Exp).then_inc(s_a, 1)
            for i in range(4):
                piece_a_hi(i)

            def head(g, j, first):
                h = g * HT + j
                act.wait_ge(s_s[j % HB], 16 * (2 * g + j // HB + 1))
                if not first:
                    act.wait_ge(s_y, h - 1)
                s.activation(toep[:, j % 2, :], s_ring[:, j % HB, ::-1], ACT.Copy).then_inc(s_r, 1)
                act.wait_ge(s_w[j % HB], 16 * (2 * g + j // HB + 1))
                s.activation(w_hi[:, bass.ds(h * WCH, WCH)], wring[:, j % HB, 0:WCH], ACT.Copy, scale=S_W)\
                    .then_inc(s_wh, 1)

            def heads(g, first):
                b_at, ad_at = SPLIT_FIRST if first else SPLIT
                for j in range(HT):
                    head(g, j, first and j < 2)
                    if j in b_at:
                        piece_b_hi(g, b_at.index(j), first)
                    if j == ad_at:
                        piece_ad_hi(g, first)

            act.wait_ge(s_k, 1)
            s.activation(ksb[0:CA, 16:32].rearrange("p h c -> p (h c)"), ps[0:CA, 5, :], ACT.Copy).then_inc(s_a, 1)
            act.wait_ge(s_kd, 32)
            heads(0, True)
            with act.Fori(1, NH // HT) as g:
                heads(g, False)

            def stage_hi_first():
                for h0, h1 in ((0, NH - HT), (NH - HT, NH)):
                    act.wait_ge(s_x1, h1)
                    last = s.activation(xstage[:, 0, 0, :, :, h0:h1].rearrange("p k b h -> p k h b"),
                                        x1[:, :, h0:h1, 0:TB], ACT.Copy, scale=S_X)
                last.then_inc(s_xh, 1)

            def stage_hi(t, par):
                wait(act, s_acc, t - 1)
                s.activation(xstage[:, par, 0].rearrange("p k b h -> p k h b"),
                             x1[:, :, :, bass.ds(t * TB, TB)], ACT.Copy, scale=S_X).then_inc(s_xh, 1)

            def pairs_turned(t, par):
                act.wait_ge(s_tp, t + 1)
                wait(act, s_gu, (t - 1) * FT)
                s.activation(t_mov[0:3 * 2 * R, par].rearrange("p g q n -> p (g q n)"),
                             ps[0:3 * 2 * R, 6, 0:2 * P].bitcast(F16), ACT.Copy).then_inc(s_tm, 1)

            def evacuate(t):
                act.wait_ge(s_acc, t + 1)
                wait(act, s_out, t * 16)
                s.activation(out_sb[:, 0, :], ps[:, 2, :], ACT.Copy, scale=1 / O_SCALE).then_inc(s_ev0, 1)

            def block_act(t, par, m):
                n = t * FT + m
                turn = (par + m) % 2
                rows = slice(0, min(P, FF - m * P))
                act.wait_ge(s_gu, n + 1)
                wait(act, s_af, n - 1)
                s.activation(sg[rows, turn], ps[rows, turn, 0:TOK], ACT.Silu, scale=1 / G_SCALE).then_inc(s_sg, 1)
                act.wait_ge(s_af, n + 1)
                wait(act, s_d, n + 1 - FT)
                s.activation(act_hl[rows, m, 0], af[rows, turn], ACT.Copy).then_inc(s_ah, 1)

            def piece_bd_hi(i):
                raw, hi, _ = piece_bd()
                act.wait_ge(s_bdi, 16 * (i + 1))
                wait(act, s_bds, 16 * 4 * i)
                s.activation(hi, raw, ACT.Copy, scale=S_W).then_inc(s_bdh, 1)

            def late_hi(i):
                c0, n = LATE[i]
                act.wait_ge(s_w[i % HB], 16 * (NH // HB + i // HB + 1))
                s.activation(w_hi[:, c0:c0 + n], wring[:, i % HB, 0:n], ACT.Copy, scale=S_W).then_inc(s_wh, 1)

            def tile(t, par, first, last):
                for m in range(FT):
                    block_act(t, par, m)
                    if first and m in BD_AT:
                        piece_bd_hi(BD_AT.index(m))
                    for d in SPLIT_AT.get(m, ()) if first else ():
                        late_hi(d)
                    if m == 2 and not first:
                        evacuate(t - 1)
                    if m == 3 and not last:
                        stage_hi(t + 1, 1 - par)
                    if m == 8 and not last:
                        pairs_turned(t + 1, 1 - par)

            stage_hi_first()
            pairs_turned(0, 0)
            tile(0, 0, True, False)
            with act.Fori(0, (NT - 2) // 2) as g:
                tile(g * 2 + 1, 1, False, False)
                tile(g * 2 + 2, 0, False, False)
            tile(NT - 1, 1, False, True)
            evacuate(NT - 1)

        @block.tensor
        def _(pe):
            mm = nc.tensor.matmul
            pe.wait_ge(s_v, V_STEP["factors"])
            for h in range(NH):
                c0 = CC * (h % 16)
                mm(ps[0:CA, 4 + h // 16, c0:c0 + CC], g1[:, h, :], fac2[:, h, :],
                   start=(h % 16 == 0), stop=False, skip_group_check=True)
            for i in range(2):
                last = mm(ps[0:CA, 4 + i, CC - 1::CC], onehot, dval[:, 16 * i:16 * i + 16],
                          start=False, stop=True, skip_group_check=True)
            last.then_inc(s_k, 1)

            def head(h, j, first):
                pe.wait_ge(s_r, h + 1)
                if not first:
                    pe.wait_ge(s_ym, h - 1)
                for lk in range(KL):
                    for mk in range(lk + 1):
                        last = mm(ps[:, j % 2, lk * P:(lk + 1) * P], toep[:, j % 2, (lk - mk) * P:(lk - mk + 1) * P],
                                  x1[:, mk, bass.ds(h, 1), :].rearrange("p a b -> p (a b)"),
                                  start=(mk == 0), stop=(mk == lk))
                last.then_inc(s_y, 1)

            pe.wait_ge(s_x, 16 * X_EARLY)
            for j in range(HB):
                head(j, j, j < 2)
            with pe.Fori(1, X_EARLY) as g:
                for j in range(HB):
                    head(g * HB + j, j, False)
            pe.wait_ge(s_x2, 16)
            for j in range(HB):
                head(X_EARLY * HB + j, j, False)

            def lora_a(t, par):
                if not (isinstance(t, int) and t == 0):
                    pe.wait_ge(s_xl, (t + 1) * KL)
                pe.wait_ge(s_ga, 16 * TB * (t + 1))
                wait(pe, s_tt, t * 2)
                if isinstance(t, int) and t == 0:
                    pe.wait_ge(s_wl, NH)
                for q in range(Q):
                    for k in range(KL):
                        if isinstance(t, int) and t == 0:
                            pe.wait_ge(s_xl, k + 1)
                        for xe, ae in ((0, 0), (0, 1), (1, 0)):
                            last = mm(ps[:, 7, q * P:(q + 1) * P],
                                      xstage[:, par, xe, k, 4 * q:4 * q + 4, :].rearrange("p b h -> p (b h)"),
                                      a_buf[:, 4 * q:4 * q + 4, ae, k, :],
                                      start=(k == 0 and xe == 0 and ae == 0), stop=(k == KL - 1 and xe == 1))
                last.then_inc(s_ta, 1)

            def turn_pairs(t):
                pe.wait_ge(s_tt, (t + 1) * 2)
                wait(pe, s_t2a, t - 1)
                for g in range(2):
                    for q in range(Q):
                        c0 = (g * Q + q) * 64
                        last = nc.tensor.transpose(ps[0:3 * 2 * R, 6, c0:c0 + 64].bitcast(F16),
                                                   tt[:, q * 2 + g].rearrange("p j n -> p (j n)"), ident[:])
                last.then_inc(s_tp, 1)

            def gate_up(t, par, m, between=None):
                n = t * FT + m
                turn = (par + m) % 2
                f = min(P, FF - m * P)
                wait(pe, s_af, n - 1)
                if isinstance(t, int) and t == 0 and m >= EARLY:
                    pe.wait_ge(s_wl, NH + sum(c < (m + 1) * WM for c, _ in LATE[:N_GU]))
                half = 1 if m * P >= FH0 else 0
                fo = m * P - half * FH0
                for g in range(2):
                    o = ps[0:f, turn, g * TOK:(g + 1) * TOK]
                    for k in range(KL):
                        c0 = m * WM + (g * KL + k) * f
                        for we, xe in ((0, 0), (0, 1), (1, 0)):
                            w = (w_hi, w_lo)[we]
                            mm(o, w[:, c0:c0 + f], xstage[:, par, xe, k].rearrange("p b h -> p (b h)"),
                               start=(k == 0 and we == 0 and xe == 0), stop=False)
                    if m == 0 and g == 0:
                        if between is not None:
                            between()
                        pe.wait_ge(s_tm, t + 1)
                    if g == 0 and m * P in (0, FH0):
                        pe.wait_ge(s_gb[half], 16 * TB * (t + 1))
                    for j in range(4):
                        last = mm(ps[0:f, turn, g * TOK + 64 * j:g * TOK + 64 * j + 64],
                                  b_half[half][0:3 * 2 * R, j, g, fo:fo + f],
                                  t_mov[0:3 * 2 * R, par, g, j // 2, 64 * (j % 2):64 * (j % 2) + 64],
                                  start=False, stop=(j == 3))
                last.then_inc(s_gu, 1)

            def down(t, m):
                kf = min(P, FF - m * P)
                pe.wait_ge(s_al, t * FT + m + 1)
                if isinstance(t, int) and t == 0:
                    pe.wait_ge(s_wl, NH + N_GU + m + 1)
                if m == 0:
                    pe.wait_ge(s_gad, 16 * TB * (t + 1))
                    wait(pe, s_ev0, t)
                    wait(pe, s_ev1, t)
                    wait(pe, s_t2, t * 4)
                for q in range(Q):
                    w = slice(WD0 + m * NL, WD0 + (m + 1) * NL)
                    for ae, we in ((0, 0), (0, 1), (1, 0)):
                        a = act_hl[0:kf, m, ae, q * P:(q + 1) * P]
                        first = m == 0 and ae == 0 and we == 0
                        mm(ps[:, 2 + q, :], a, (w_hi, w_lo)[we][0:kf, w], start=first, stop=False)
                        last = mm(ps[:, 4 + q, 0:4 * R], a, ad_buf[0:kf, 4 * q:4 * q + 4, we, m, :],
                                  start=first, stop=(m == FT - 1 and ae == 1))
                last.then_inc(s_d, 1)

            def turn_down(t):
                pe.wait_ge(s_t2, (t + 1) * 4)
                wait(pe, s_tm, t + 1)
                for q in range(Q):
                    last = nc.tensor.transpose(ps[:, 6, q * 64:q * 64 + 64].bitcast(F16), t2[:, q, :], ident[:])
                last.then_inc(s_t2p, 1)

            def residual(par):
                for q in range(Q):
                    for k in range(KL):
                        for e in range(2):
                            mm(ps[:, 2 + q, k * P:(k + 1) * P],
                               xstage[:, par, e, k, 4 * q:4 * q + 4, :].rearrange("p b h -> p (b h)"),
                               ident_x[:], start=False, stop=False)

            def finish(t):
                pe.wait_ge(s_t2a, t + 1)
                pe.wait_ge(s_gbd, 16 * TB * (t + 1))
                for q in range(Q):
                    for e in range(2):
                        last = mm(ps[:, 2 + q, :], t2a[:, q, :], bd_buf[:, q, e, :], start=False, stop=(e == 1))
                last.then_inc(s_acc, 1)

            def tile(t, par, first, last):
                for m in range(FT):
                    gate_up(t, par, m, (lambda: turn_pairs(0)) if first and m == 0 else None)
                    if not first:
                        if m == 0:
                            down(t - 1, FT - 1)
                        if m == 1:
                            turn_down(t - 1)
                        if m == 2:
                            residual(1 - par)
                            finish(t - 1)
                    if m == 6 and not last:
                        lora_a(t + 1, 1 - par)
                    if m == 8 and not last:
                        turn_pairs(t + 1)
                    for d in (DOWN_AT_0 if first else DOWN_AT).get(m, ()):
                        down(t, d)

            DOWN_AT_0 = {9: (0, 1, 2, 3), 10: (4, 5, 6, 7, 8, 9)}
            DOWN_AT = {4: (0, 1, 2), 5: (3, 4), 6: (5,), 7: (6,), 8: (7,), 9: (8,), 10: (9,)}
            lora_a(0, 0)
            tile(0, 0, True, False)
            pe.wait_ge(s_wl, NH + len(LATE))
            with pe.Fori(0, (NT - 2) // 2) as g:
                tile(g * 2 + 1, 1, False, False)
                tile(g * 2 + 2, 0, False, False)
            tile(NT - 1, 1, False, True)
            down(NT - 1, FT - 1)
            residual(1)
            turn_down(NT - 1)
            finish(NT - 1)

        @block.sync
        def _(sp):
            sp.dma_start(params, par).then_inc(s_par, 16)
            sp.dma_start(dval, dvec.unsqueeze(0)).then_inc(s_par, 16)
            sp.dma_start(leni, length.partition_broadcast(P)).then_inc(s_par, 16)
            sp.dma_start(adapter_sb[:], adapter).then_inc(s_par, 16)
            for i in range(4):
                sp.dma_start(piece_a(i)[0], lora[:, NLA * i:NLA * (i + 1)]).then_inc(s_ai[i], 16)

            def x_load(q, s):
                sp.dma_start(x1[:, :, q * HB:(q + 1) * HB, :],
                             xt[:, q].rearrange("p k (h b) -> p k h b", h=HB)).then_inc(s, 16)

            for q in range(X_EARLY):
                x_load(q, s_x)

            def indices(t):
                return [sp.value_load(adapter_sb[:, bass.ds(t * TB + j, 1)], min_val=0, max_val=NAD - 1)
                        for j in range(TB)]

            def fetch_a(t, idx):
                wait(sp, s_ta, t)
                for j, a in enumerate(idx):
                    sp.dma_start(a_buf[:, j].rearrange("p e k n -> p e (k n)"),
                                 a_scr[bass.ds(a, 1)].squeeze(0)).then_inc(s_ga, 16)

            def strip_load(h, slot, first):
                if not first:
                    sp.wait_ge(s_r, h - HB + 1)
                sp.dma_start(s_ring[:, slot, :], strip(h)).then_inc(s_s[slot], 16)

            def weight_load(h, slot, first):
                if not first:
                    sp.wait_ge(s_wl, h - HB + 1)
                sp.dma_start(wring[:, slot, 0:WCH], wall[:, bass.ds(h * WCH, WCH)]).then_inc(s_w[slot], 16)

            def strip(h):
                return bass.AP(krev.tensor, h * KROW, [[1, P], [1, NL]])

            def load_b(g, blk, first):
                src = lora[:, bass.ds(g * NLB + OFF_B + 4 * NLB * blk, NLB)]
                if not first:
                    sp.wait_ge(s_bl, g * 2 + blk - 1)
                sp.dma_start(piece_b(blk)[0], src).then_inc(s_bi[blk], 16)

            def store_b(g, blk):
                _, hi, lo = piece_b(blk)
                col = g * NLB
                sp.wait_ge(s_bl, g * 2 + blk + 1)
                for e, src in ((2, lo), (1, hi), (0, hi)):
                    dst = bass.AP(b_scr.tensor, col + (24 * blk + e) * R * 2 * FF,
                                  [[3 * R * 2 * FF, 8], [2 * FF, R], [1, NLB]])
                    sp.dma_start(dst, src).then_inc(s_bs[blk], 16)

            def load_ad(g, first):
                src = lora[:, bass.ds(g * NLD + OFF_AD, NLD)]
                if not first:
                    sp.wait_ge(s_adl, g)
                sp.dma_start(piece_ad()[0], src).then_inc(s_adi, 16)

            def store_ad(g):
                _, hi, lo = piece_ad()
                row = g * (4 * P * 2 * FT * R)
                sp.wait_ge(s_adl, g + 1)
                for e, src in ((1, lo), (0, hi)):
                    dst = bass.AP(ad_scr.tensor, row + e * FT * R, [[2 * FT * R, P], [P * 2 * FT * R, 4], [1, FT * R]])
                    sp.dma_start(dst, src.rearrange("p (a n) -> p a n", a=4)).then_inc(s_ads, 16)

            def store_a():
                for i in range(4):
                    sp.wait_ge(s_al0, i + 1)
                    for e, src in enumerate(piece_a(i)[1:]):
                        sp.dma_start(a_scr[4 * i:4 * i + 4, :, e, :].rearrange("a p n -> p a n"),
                                     src.rearrange("p (a n) -> p a n", a=4)).then_inc(s_as, 16)

            def heads(g, first):
                for j in range(HT):
                    strip_load(g * HT + j, j % HB, first and j < HB)
                    if not first or j >= HB:
                        weight_load(g * HT + j, j % HB, False)
                    if first and j == HB - 1:
                        store_a()
                    if first and j == HB + 1:
                        sp.wait_ge(s_as, 16 * 8)
                        for blk in range(2):
                            load_b(0, blk, True)
                    if not first:
                        if j in (0, 2):
                            store_b(g - 1, j // 2)
                        if j in (1, 3):
                            load_b(g, j // 2, False)
                        if j == 4:
                            store_ad(g - 1)
                    if j == (HT - 1 if first else 5):
                        load_ad(g, first)
                    if first and j == HT - 1:
                        x_load(X_EARLY, s_x2)

            for h in range(HB):
                weight_load(h, h, True)
            sp.wait_ge(s_pool, 1)
            sp.dma_start(krev[:, NL:KROW], zrow).then_inc(s_kd, 16)
            sp.wait_ge(s_par, 16 * NPAR)
            adapters = indices(0)
            sp.wait_ge(s_v, V_KSB[0])
            sp.wait_ge(s_a, 6)
            sp.dma_start(krev[:, 0:NL].rearrange("h (a c) -> a h c", a=CA), ksb[0:CA]).then_inc(s_kd, 16)
            sp.wait_ge(s_kd, 32)

            heads(0, True)
            fetch_a(0, adapters)
            with sp.Fori(1, NH // HT) as g:
                heads(g, False)
            for blk in range(2):
                store_b(NH // HT - 1, blk)
            for blk in range(2):
                sp.wait_ge(s_bs[blk], 16 * 3 * 4)

            def fetch_b(t, idx, half, prev):
                if prev:
                    sp.wait_ge(s_gu, (t - 1) * FT + (FH0 // P if half == 0 else FT))
                f0 = FH0 * half
                for j, a in enumerate(idx):
                    r0 = 3 * R * (j % 2)
                    sp.dma_start(b_half[half][r0:r0 + 3 * R, j // 2],
                                 b_scr[bass.ds(a, 1), :, :, :, f0:f0 + FHS[half]]
                                 .rearrange("a e r g f -> (a e r) g f")).then_inc(s_gb[half], 16)

            def fetch_ad(t, idx, prev):
                if prev:
                    sp.wait_ge(s_d, t * FT)
                else:
                    sp.wait_ge(s_ads, 16 * 2 * 4)
                for j, a in enumerate(idx):
                    sp.dma_start(ad_buf[:, j].rearrange("p e k n -> p e (k n)"),
                                 ad_scr[bass.ds(a, 1)].squeeze(0)).then_inc(s_gad, 16)

            def fetch_bd(t, idx, prev):
                if prev:
                    sp.wait_ge(s_acc, t)
                else:
                    sp.wait_ge(s_bds, 16 * 4 * 2)
                for j, a in enumerate(idx):
                    r0 = 2 * R * (j % 4)
                    sp.dma_start(bd_buf[r0:r0 + 2 * R, j // 4],
                                 bd_scr[bass.ds(a, 1)].rearrange("a e r g f -> (a e r) g f")).then_inc(s_gbd, 16)

            def load_late(i):
                c0, n = LATE[i]
                sp.wait_ge(s_wl, NH + i + 1 - HB)
                sp.dma_start(wring[:, i % HB, 0:n], wall[:, c0:c0 + n]).then_inc(s_w[i % HB], 16)

            def store(t):
                sp.wait_ge(s_ev0, t + 1)
                sp.wait_ge(s_ev1, t + 1)
                sp.dma_start(out[bass.ds(t * TOK, TOK), :].rearrange("(q p) n -> p q n", q=Q), out_sb[:])\
                    .then_inc(s_out, 16)

            fetch_b(0, adapters, 0, False)
            store_ad(NH // HT - 1)
            for i in range(HB):
                load_late(i)
            fetch_b(0, adapters, 1, False)
            second = indices(1)
            fetch_a(1, second)
            BEFORE_AD = 11
            for i in range(HB, BEFORE_AD):
                load_late(i)
            fetch_ad(0, adapters, False)
            for i in range(BEFORE_AD, len(LATE)):
                load_late(i)
            fetch_b(1, second, 0, True)
            fetch_bd(0, adapters, False)
            fetch_b(1, second, 1, True)
            fetch_ad(1, second, True)
            fetch_bd(1, second, True)
            with sp.Fori(2, NT) as t:
                idx = indices(t)
                store(t - 2)
                fetch_a(t, idx)
                fetch_b(t, idx, 0, True)
                fetch_b(t, idx, 1, True)
                fetch_ad(t, idx, True)
                fetch_bd(t, idx, True)
            store(NT - 2)
            store(NT - 1)
            sp.wait_ge(s_out, 16 * NT)

        @block.gpsimd
        def _(pool):
            g = nc.gpsimd
            g.memset(zrow, 0.0).then_inc(s_pool, 1)
            g.iota(lags[:, 0:CA], [[-CC, CA]], base=CC * (CA - 1), channel_multiplier=0,
                   allow_small_or_imprecise_dtypes=True).then_inc(s_pool, 1)
            g.iota(lags[:, FAC2], [[-1, CC]], base=CC - 1, channel_multiplier=0,
                   allow_small_or_imprecise_dtypes=True).then_inc(s_pool, 1)
            g.memset(lags[:, STEP:STEP + 1], 1.0).then_inc(s_pool, 1)
            g.iota(ioti.rearrange("p (k b) -> p k b", k=KL), [[P, KL], [0, NB]], base=0, channel_multiplier=1,
                   allow_small_or_imprecise_dtypes=True).then_inc(s_pool, 1)
            g.memset(onehot, 0.0).then_inc(s_pool, 1)
            g.memset(ident[:], 0.0).then_inc(s_pool, 1)
            g.memset(ident_x[:], 0.0).then_inc(s_pool, 1)
            g.memset(tt[:], 0.0).then_inc(s_pool, 1)
            g.memset(t2[:], 0.0).then_inc(s_pool, 1)
            pool.wait_ge(s_pool, 10)
            g.memset(onehot[:, CA - 1:CA], 1.0).then_inc(s_pool, 1)
            for m, v in ((ident, 1.0), (ident_x, O_SCALE / S_X)):
                g.affine_select(out=m[:], in_=m[:], compare_op=ALU.not_equal, fill=v, base=0,
                                pattern=[[-1, P]], channel_multiplier=1).then_inc(s_pool, 1)
            g.memset(half_pi[:], TWO_PI / 4).then_inc(s_pool, 1)

            steps = [0]

            def step(ins):
                steps[0] += 1
                ins.then_inc(s_g, 1)
                pool.wait_ge(s_g, steps[0])

            pool.wait_ge(s_par, 16 * NPAR)
            step(g.tensor_scalar(term(a4, 0, 1), a_im, 1.0, None, ALU.mult))
            step(g.tensor_scalar(term(a4, 1, 0), a_im, -1.0, None, ALU.mult))
            top, low = slice(0, NST), slice(NST, 2 * NST)
            for half, out, c_of_re, f_re, c_of_im, f_im in (
                    (top, 0, c_re, 2.0, c_im, -2.0), (top, 1, c_im, -2.0, c_re, -2.0),
                    (low, 0, c_im, -2.0, c_re, -2.0), (low, 1, c_re, -2.0, c_im, 2.0)):
                step(g.tensor_scalar(term(c4, out, 0)[half], c_of_re[half], f_re, None, ALU.mult))
                step(g.tensor_scalar(term(c4, out, 1)[half], c_of_im[half], f_im, None, ALU.mult))

            pool.wait_ge(s_v, V_STEP["d_re"])
            step(g.tensor_scalar(eg_k, d_re, 1 / LN2, -125.0, ALU.mult, ALU.max))
            step(g.tensor_scalar(eg_k, eg_k, 126.0, MAGIC, ALU.min, ALU.add))
            step(g.tensor_scalar(eg_k, eg_k, MAGIC, None, ALU.subtract))
            for part in (LN2_HI, LN2_LO):
                step(g.tensor_scalar(eg_u, eg_k, -part, None, ALU.mult))
                step(g.tensor_tensor(eg_r, eg_u, d_re if part == LN2_HI else eg_r, ALU.add))
            step(g.tensor_scalar(eg_p, eg_r, EXP_C[0], EXP_C[1], ALU.mult, ALU.add))
            for c in EXP_C[2:]:
                step(g.tensor_tensor(eg_p, eg_p, eg_r, ALU.mult))
                step(g.tensor_scalar(eg_p, eg_p, c, None, ALU.add))
            step(g.tensor_scalar(eg_o.bitcast(I32), eg_k, 127.0, 8388608.0, ALU.add, ALU.mult))
            step(g.tensor_tensor(eg_o, eg_p, eg_o, ALU.mult))
            assert steps[0] == G_STEP["exp"], steps
            step(g.tensor_tensor(mag_t, d_re.unsqueeze(2).to_broadcast([P, NH, NE]),
                                 lags.unsqueeze(1).to_broadcast([P, NH, NE]), ALU.mult))

            for i in range(4):
                raw, hi, lo = piece_a(i)
                pool.wait_ge(s_ah0, 2 * (i + 1))
                g.tensor_tensor(lo, raw, hi, ALU.subtract).then_inc(s_al0, 1)

            pool.wait_ge(s_y, NH)
            for i in range(2):
                wait(pool, s_bds, 16 * 4 * i)
                pool.dma_start(piece_bd()[0], lora[:, OFF_BD + i * NL:OFF_BD + (i + 1) * NL]).then_inc(s_bdi, 16)
                pool.wait_ge(s_bdl, i + 1)
                _, hi, lo = piece_bd()
                for d in range(2):
                    for e, src in enumerate((hi, lo)):
                        pool.dma_start(bd_scr[8 * i:8 * i + 8, d, :, e, :], src).then_inc(s_bds, 16)


def kernel(x, itok_B_78_3631, itok_B_2_6, L0_cond_log_dt, L0_cond_C, L0_cond_log_A_real, L0_cond_A_imag, L0_cond_D,
           L1_cond_W_gate, L1_cond_W_up, L1_cond_W_down, L1_cond_A_gate, L1_cond_B_gate, L1_cond_A_up,
           L1_cond_B_up, L1_cond_A_down, L1_cond_B_down):
    import numpy as np
    import concourse.bacc as bacc
    from concourse.bass_utils import run_bass_kernel_spmd

    def arr(a):
        return np.asarray(a)

    xt = arr(x).transpose(2, 1, 0).reshape(KL, P, NH // 4, 4 * NB).transpose(1, 2, 0, 3)
    wall = np.zeros((P, NW), np.float32)
    gu = np.stack([arr(w).T.reshape(KL, P, FF).transpose(1, 0, 2) for w in (L1_cond_W_gate, L1_cond_W_up)], axis=1)
    for m in range(FT):
        block = gu[..., m * P:(m + 1) * P].reshape(P, -1)
        wall[:, m * WM:m * WM + block.shape[1]] = block
    wd = np.zeros((FT * P, NL), np.float32)
    wd[:FF] = arr(L1_cond_W_down).T
    wall[:, WD0:] = wd.reshape(FT, P, NL).transpose(1, 0, 2).reshape(P, FT * NL)
    a_gu = np.stack([arr(L1_cond_A_gate)[0], arr(L1_cond_A_up)[0]])
    a_gu = a_gu.reshape(2, NAD, R, KL, P).transpose(4, 1, 3, 0, 2).reshape(P, 4, NLA)
    parts = [a_gu[:, i] for i in range(4)]
    b_t = [arr(b)[0].transpose(0, 2, 1).reshape(NAD * R, FF) for b in (L1_cond_B_gate, L1_cond_B_up)]
    parts += [b_t[gu][blk * P:(blk + 1) * P] for blk in range(2) for gu in range(2)]
    ad = np.zeros((NAD, R, FT * P), np.float32)
    ad[:, :, :FF] = arr(L1_cond_A_down)[0]
    ad = ad.reshape(NAD, R, FT, P).transpose(3, 0, 2, 1).reshape(P, 4, 4 * FT * R)
    bd = arr(L1_cond_B_down)[0].transpose(0, 2, 1).reshape(2, P, NL)
    parts += [ad[:, i] for i in range(4)] + [bd[0], bd[1]]
    c = arr(L0_cond_C)
    par = [np.broadcast_to(arr(L0_cond_log_dt), (NST, NH)), arr(L0_cond_log_A_real).T, arr(L0_cond_A_imag).T,
           c[:, :, 0].T, c[:, :, 1].T]
    par = np.tile(np.concatenate(par, axis=1), (2, 1))
    ins = {
        "xt": xt, "wall": wall, "lora": np.concatenate(parts, axis=1),
        "par": par, "dvec": arr(L0_cond_D),
        "length": arr(itok_B_78_3631), "adapter": arr(itok_B_2_6).reshape(1, NB),
    }
    nc = bacc.Bacc("TRN2", target_bir_lowering=False, num_devices=1)
    arrays, aps = {}, {}
    for name, a in ins.items():
        a = np.ascontiguousarray(a)
        arrays[name] = a
        aps[name] = nc.dram_tensor(name, a.shape, mybir.dt.from_np(a.dtype), kind="ExternalInput").ap()
    y = nc.dram_tensor("y", (NB * NH, NL), F32, kind="ExternalOutput").ap()
    build(nc, out=y, **aps)
    r = run_bass_kernel_spmd(nc, [arrays], core_ids=[0])
    return r.results[0]["y"].reshape(NB, NH, NL)
```
